# Optimizing a Trainium2 kernel written in Bass

```python
import numpy as np
import jax
import jax.numpy as jnp

def _softmax(x, axis=-1):
    return jax.nn.softmax(x, axis=axis)

def _gelu(x):
    return jax.nn.gelu(x, approximate=True)

def _silu(x):
    return jax.nn.silu(x)

def _sigmoid(x):
    return jax.nn.sigmoid(x)

def _layernorm(x, axis=-1, eps=1e-05):
    m = jnp.mean(x, axis=axis, keepdims=True)
    v = jnp.var(x, axis=axis, keepdims=True)
    return (x - m) / jnp.sqrt(v + eps)

def _scatter_add(tgt, idx, src, axis=0):
    return tgt.at[idx].add(src)

def _segment_sum(src, seg, n):
    return jax.ops.segment_sum(src, seg, n)
kernel_name = 'mk_audio_tower_d1_tok_audfeat768_r4_c40f69'

def setup_inputs(seed: int=0):
    np.random.seed(seed)
    _w = jnp.asarray

    def _rec_inputs():
        import jax
        import jax.numpy as jnp
        _rk = jax.random.key(seed)
        x = -0.000147625 + 0.999875 * jax.random.normal(jax.random.fold_in(_rk, 1), (64, 256, 192), jnp.float32)
        return x
    x = _rec_inputs()

    def _L0_tok_setup():
        import jax, jax.numpy as jnp
        import numpy as np
        T = 16
        N = 196
        B = 16
        D = 192
        key = jax.random.key(seed)
        k1, k2, k3, k4, k5 = jax.random.split(key, 5)
        return {'x': jax.random.normal(k1, (N, B * T, D), dtype=jnp.float32), 'Wq': jax.random.normal(k2, (T // 2, T), dtype=jnp.float32) * 0.25, 'bq': jax.random.normal(k3, (T // 2,), dtype=jnp.float32) * 0.02, 'Wkv': jax.random.normal(k4, (T, T), dtype=jnp.float32) * 0.25, 'bkv': jax.random.normal(k5, (T // 2,), dtype=jnp.float32) * 0.02}
    _L0_tok_all = _L0_tok_setup()
    _L0_tok_in = {k: v for k, v in _L0_tok_all.items() if k in ('Wq', 'bq', 'Wkv', 'bkv')}
    del _L0_tok_all

    def _L0_attn_setup():
        import jax, jax.numpy as jnp
        import numpy as np
        N_HEAD = 12
        N_KV_HEADS = 3
        KV_REPEAT = 4
        HEAD_DIM = 64
        BLOCK = 256
        SCALE = (HEAD_DIM * 4 / 12) ** (-0.5)
        ROPE_BASE = 10000.0

        def rope_cos_sin(T, d):
            inv_freq = 1.0 / ROPE_BASE ** (jnp.arange(0, d, 2, dtype=jnp.float32) / d)
            t = jnp.arange(T, dtype=jnp.float32)
            freqs = jnp.outer(t, inv_freq)
            return (jnp.cos(freqs), jnp.sin(freqs))

        def apply_rope(x, cos, sin):
            d = x.shape[-1] // 2
            x1, x2 = (x[..., :d], x[..., d:])
            c = cos[None, None]
            s = sin[None, None]
            return jnp.concatenate([x1 * c + x2 * s, -x1 * s + x2 * c], axis=-1)
        key = jax.random.key(seed)
        ks = jax.random.split(key, 5)
        B, T, E = (1, 768, 192)
        x = jax.random.normal(ks[0], (B, T, E), dtype=jnp.float32)
        w = 1.0 / np.sqrt(E)
        Wq = jax.random.normal(ks[1], (E, N_HEAD * HEAD_DIM), dtype=jnp.float32) * w
        Wk = jax.random.normal(ks[2], (E, N_KV_HEADS * HEAD_DIM), dtype=jnp.float32) * w
        Wv = jax.random.normal(ks[3], (E, N_KV_HEADS * HEAD_DIM), dtype=jnp.float32) * w
        Wo = jax.random.normal(ks[4], (N_HEAD * HEAD_DIM, E), dtype=jnp.float32) * w
        return {'x': x, 'Wq': Wq, 'Wk': Wk, 'Wv': Wv, 'Wo': Wo}
    _L0_attn_all = _L0_attn_setup()
    _L0_attn_in = {k: v for k, v in _L0_attn_all.items() if k in ('Wq', 'Wk', 'Wv', 'Wo')}
    del _L0_attn_all

    def _L0_ffn_setup():
        import jax, jax.numpy as jnp
        import numpy as np
        B, S, D_IN, D_HID, D_OUT = (32, 128, 192, 768, 192)
        key = jax.random.key(seed)
        k1, k2, k3, k4 = jax.random.split(key, 4)
        init_k = float(np.sqrt(1.0 / D_IN))
        init_k2 = float(np.sqrt(1.0 / D_HID))
        x = jax.random.normal(k1, (B, S, D_IN), dtype=jnp.float32)
        in_weight = jax.random.uniform(k2, (D_HID, D_IN), dtype=jnp.float32, minval=-init_k, maxval=init_k)
        in_bias = jax.random.uniform(k3, (D_HID,), dtype=jnp.float32, minval=-init_k, maxval=init_k)
        out_weight = jax.random.uniform(k4, (D_HID, D_OUT), dtype=jnp.float32, minval=-init_k2, maxval=init_k2)
        return {'x': x, 'in_weight': in_weight, 'in_bias': in_bias, 'out_weight': out_weight}
    _L0_ffn_all = _L0_ffn_setup()
    _L0_ffn_in = {k: v for k, v in _L0_ffn_all.items() if k in ('in_weight', 'in_bias', 'out_weight')}
    del _L0_ffn_all
    return {'x': x, 'L0_tok_Wq': _L0_tok_in['Wq'], 'L0_tok_bq': _L0_tok_in['bq'], 'L0_tok_Wkv': _L0_tok_in['Wkv'], 'L0_tok_bkv': _L0_tok_in['bkv'], 'L0_attn_Wq': _L0_attn_in['Wq'], 'L0_attn_Wk': _L0_attn_in['Wk'], 'L0_attn_Wv': _L0_attn_in['Wv'], 'L0_attn_Wo': _L0_attn_in['Wo'], 'L0_ffn_in_weight': _L0_ffn_in['in_weight'], 'L0_ffn_in_bias': _L0_ffn_in['in_bias'], 'L0_ffn_out_weight': _L0_ffn_in['out_weight']}

def reference(x, L0_tok_Wq, L0_tok_bq, L0_tok_Wkv, L0_tok_bkv, L0_attn_Wq, L0_attn_Wk, L0_attn_Wv, L0_attn_Wo, L0_ffn_in_weight, L0_ffn_in_bias, L0_ffn_out_weight):
    import jax
    import jax.numpy as jnp

    def _L0_tok_ref(x, Wq, bq, Wkv, bkv):
        import jax, jax.numpy as jnp
        import numpy as np
        T = 16
        N = 196
        B = 16
        D = 192
        n, bt, d = x.shape
        t = Wkv.shape[0]
        b = bt // t
        t2 = t // 2
        scale = 1.0 / np.sqrt(d).astype(np.float32)
        xv = x.reshape(n, b, t, d).transpose(1, 0, 3, 2)
        q = jnp.einsum('bndt,st->bnds', xv, Wq) + bq
        kv_bias = jnp.concatenate([jnp.zeros_like(bkv), bkv])
        kv = jnp.einsum('bndt,st->bnds', xv, Wkv) + kv_bias
        kv = kv.reshape(b, n, d, 2, t2)
        k = kv[:, :, :, 0, :]
        v = kv[:, :, :, 1, :]
        q = q * scale
        attn = jax.nn.softmax(jnp.einsum('bnds,bndr->bnsr', q, k), axis=-1)
        out = q.transpose(0, 1, 3, 2) + jnp.einsum('bnsr,bndr->bnsd', attn, v)
        return out.transpose(1, 0, 2, 3).reshape(n, b * t2, d)

    def _L0_attn_ref(x, Wq, Wk, Wv, Wo):
        import jax, jax.numpy as jnp
        import numpy as np
        N_HEAD = 12
        N_KV_HEADS = 3
        KV_REPEAT = 4
        HEAD_DIM = 64
        BLOCK = 256
        SCALE = (HEAD_DIM * 4 / 12) ** (-0.5)
        ROPE_BASE = 10000.0

        def rope_cos_sin(T, d):
            inv_freq = 1.0 / ROPE_BASE ** (jnp.arange(0, d, 2, dtype=jnp.float32) / d)
            t = jnp.arange(T, dtype=jnp.float32)
            freqs = jnp.outer(t, inv_freq)
            return (jnp.cos(freqs), jnp.sin(freqs))

        def apply_rope(x, cos, sin):
            d = x.shape[-1] // 2
            x1, x2 = (x[..., :d], x[..., d:])
            c = cos[None, None]
            s = sin[None, None]
            return jnp.concatenate([x1 * c + x2 * s, -x1 * s + x2 * c], axis=-1)
        B, T, E = x.shape
        q = (x @ Wq).reshape(B, T, N_HEAD, HEAD_DIM).transpose(0, 2, 1, 3)
        k = (x @ Wk).reshape(B, T, N_KV_HEADS, HEAD_DIM).transpose(0, 2, 1, 3)
        v = (x @ Wv).reshape(B, T, N_KV_HEADS, HEAD_DIM).transpose(0, 2, 1, 3)
        k = jnp.repeat(k, KV_REPEAT, axis=1)
        v = jnp.repeat(v, KV_REPEAT, axis=1)
        cos, sin = rope_cos_sin(T, HEAD_DIM)
        q = apply_rope(q, cos, sin)
        k = apply_rope(k, cos, sin)
        scores = jnp.einsum('bhqd,bhkd->bhqk', q, k) * jnp.float32(SCALE)
        i = jnp.arange(T)
        start = jnp.clip(i - BLOCK // 2, 0, T - BLOCK)
        j = jnp.arange(T)
        valid = (j[None, :] >= start[:, None]) & (j[None, :] < start[:, None] + BLOCK)
        scores = jnp.where(valid[None, None], scores, jnp.float32(-1e+30))
        attn = jax.nn.softmax(scores, axis=-1)
        out = jnp.einsum('bhqk,bhkd->bhqd', attn, v)
        out = out.transpose(0, 2, 1, 3).reshape(B, T, N_HEAD * HEAD_DIM)
        return out @ Wo

    def _L0_ffn_ref(x, in_weight, in_bias, out_weight):
        import jax, jax.numpy as jnp
        import numpy as np
        B, S, D_IN, D_HID, D_OUT = (32, 128, 192, 768, 192)
        lead = x.shape[:-1]
        xt = x.reshape(-1, in_weight.shape[1])
        h = jax.nn.gelu(jnp.einsum('td,hd->th', xt, in_weight) + in_bias, approximate=False)
        out = jnp.einsum('th,ho->to', h, out_weight)
        return out.reshape(*lead, out_weight.shape[1])
    h = _L0_tok_ref(x, L0_tok_Wq, L0_tok_bq, L0_tok_Wkv, L0_tok_bkv)
    h = h + _L0_attn_ref(_layernorm(h, axis=-1), L0_attn_Wq, L0_attn_Wk, L0_attn_Wv, L0_attn_Wo)
    h = h + _L0_ffn_ref(_layernorm(h, axis=-1), L0_ffn_in_weight, L0_ffn_in_bias, L0_ffn_out_weight)
    return h

_drawn_inputs = setup_inputs


def setup_inputs(seed=0):
    import zlib

    import numpy as np

    out = dict(_drawn_inputs(seed))
    spreads = {}
    factors = {'L0_tok_bq': 3.845, 'L0_ffn_in_bias': 3.291}
    for name, (base, spread) in spreads.items():
        noise = np.random.default_rng([zlib.crc32(name.encode()), seed]).standard_normal(out[name].shape)
        drawn = base * np.exp(spread * noise) if base else spread * noise
        out[name] = jnp.asarray(drawn.astype(out[name].dtype))
    for name, factor in factors.items():
        out[name] = (out[name] * factor).astype(out[name].dtype)
    return out
```

```python
from contextlib import ExitStack

import numpy as np

import concourse.bass as bass
from concourse import mybir

ALU = mybir.AluOpType
ACT = mybir.ActivationFunctionType
F32 = mybir.dt.float32
F32R = mybir.dt.float32r
BF16 = mybir.dt.bfloat16
AX_X = mybir.AxisListType.X

P = 128
D = 192
D2 = D - P
DP = 2 * P
T = 16
T2 = T // 2
NH, NKV, HD = 12, 3, 64
REP = NH // NKV
DQ, DKV = NH * HD, NKV * HD
BANKW = 384
HALF = HD // 2
HID = 768
NM = HID // P
SCALE = float(np.float32((HD * 4 / 12) ** -0.5))
TOK_SCALE = float(np.float32(1.0) / np.sqrt(np.float32(D)))
EPS = 1e-5
NEG = -1e30


def const_tables():
    inv = (1.0 / np.power(np.float32(10000.0), np.arange(0, HD, 2, dtype=np.float32) / np.float32(HD))).astype(np.float32)
    fr = np.outer(np.arange(P, dtype=np.float32), inv).astype(np.float32)
    cos, sin = np.cos(fr).astype(np.float32), np.sin(fr).astype(np.float32)
    row = np.arange(P)
    blk = (row[:, None] // T2 == row[None, :] // T2)
    return {
        "ident": np.eye(P, dtype=np.float32),
        "rope_c": np.concatenate([cos, cos], 1),
        "rope_s": np.concatenate([sin, -sin], 1),
        "score_mask": np.where(blk, 0.0, NEG).astype(np.float32),
        "block_ones": (row[:, None] // T == np.arange(P // 2)[None, :] // T2).astype(np.float32),
        "head_sel": np.repeat(np.eye(NH, dtype=np.float32), P, axis=1),
    }


def program(nc, x, w_tok, b_tok, bq_row, w_att1, w_att2, wo, w_in1, w_in2, b_in, w_out,
            c_ident, c_rope_c, c_rope_s, c_mask, c_blk, c_sel, out):
    NSEQ = x.shape[0]
    NP = NSEQ // 2

    with ExitStack() as ctx:
        def sb(name, shape, dt=F32):
            return ctx.enter_context(nc.sbuf_tensor(name, shape, dt))

        def sem(name):
            return ctx.enter_context(nc.semaphore(name))

        RING = [ctx.enter_context(nc.psum_tensor(f"ring{a}", [P, 1536], F32)) for a in range(2)]
        B6 = ctx.enter_context(nc.psum_tensor("bank6", [P, 512], F32))
        B7 = ctx.enter_context(nc.psum_tensor("bank7", [P, 512], F32))

        ident, rope_c, rope_s = sb("ident", [P, P]), sb("rope_c", [P, HD]), sb("rope_s", [P, HD])
        smask, blk = sb("smask", [P, P]), sb("blk", [P, P // 2])
        sel_f, sel = sb("sel_f", [NH, NH * P]), sb("sel", [P, NH * P], BF16)
        half_neg = sb("half_neg", [P, 2])
        wrep = sb("wrep", [P, 3, T2])
        bd_qk, bd_v = sb("bd_qk", [P, P]), sb("bd_v", [P, P // 2])
        bqk_row, bias_rows = sb("bqk_row", [P, DP]), sb("bias_rows", [P, 2])
        bias_sc = sb("bias_sc", [P, 1])
        w_raw1, w_raw2 = sb("w_raw1", [P, 1152]), sb("w_raw2", [P, 1152])
        WH1, WL1, W2S = (sb(n, [P, 1152], F32R) for n in ("WH1", "WL1", "W2S"))
        wo_sb = sb("wo_sb", [P, NM, D])
        win_raw = sb("win_raw", [P, 2 * HID])
        FH1, FL1, F2S = (sb(n, [P, HID], F32R) for n in ("FH1", "FL1", "F2S"))
        b_hid, wout_sb = sb("b_hid", [P, NM]), sb("wout_sb", [P, NM, D])

        x_sb = sb("x_sb", [P, 2, 2, D])
        qkT1, qkT2 = sb("qkT1", [P, 2, DP]), sb("qkT2", [D2, 2, DP])
        t_s, t_e, t_a, t_aT = (sb(n, [P, 2, P]) for n in ("t_s", "t_e", "t_a", "t_aT"))
        t_max, t_neg, t_sum, t_rs = (sb(n, [P, 2]) for n in ("t_max", "t_neg", "t_sum", "t_rs"))
        t_v, h_next, h_cur = (sb(n, [P, 2, D]) for n in ("t_v", "h_next", "h_cur"))
        st1, mv1, ve1, rs1 = sb("st1", [P, 2, 6]), sb("mv1", [P, 2, 2]), sb("ve1", [P, 2]), sb("rs1", [P, 2])
        xn = sb("xn", [P, 2, DP])
        XH, XL = sb("XH", [P, 2, DP], F32R), sb("XL", [P, 2, DP], F32R)
        rot_c, rot_s = sb("rot_c", [P, 2, DQ + DKV]), sb("rot_s", [P, 2, DQ + DKV])
        q_tok, k_tok = sb("q_tok", [P, 2, DQ]), sb("k_tok", [P, 2, NKV, 2, HD])
        QH, QL = sb("QH", [P, 2, DQ], F32R), sb("QL", [P, 2, DQ], F32R)
        KH, KL = sb("KH", [P, 2, NKV, 2 * P], F32R), sb("KL", [P, 2, NKV, 2 * P], F32R)
        m_q, negmT = sb("m_q", [P, 2, NH]), sb("negmT", [P, 2, P], BF16)
        E = sb("E", [P, 2, NKV, 512])
        v1 = sb("v1", [P, 2, NKV, HD + 1])
        rden, O_sb, OT = sb("rden", [P, 2, 2, 6]), sb("O_sb", [P, 2, DQ]), sb("OT", [P, 2, DQ])
        h2 = sb("h2", [P, 2, D])
        st2, mv2, ve2, rs2 = sb("st2", [P, 2, 6]), sb("mv2", [P, 2, 2]), sb("ve2", [P, 2]), sb("rs2", [P, 2])
        hn = sb("hn", [P, 2, DP])
        HH, HL = sb("HH", [P, 2, 2, P], F32R), sb("HL", [P, 2, 2, P], F32R)
        G, out_sb = sb("G", [P, NM, 2 * P]), sb("out_sb", [P, 2, D])

        s_const, s_w1, s_w2, s_w3 = sem("s_const"), sem("s_w1"), sem("s_w2"), sem("s_w3")
        s_scaled, s_bd, s_split, s_zero, s_sel = (
            sem(n) for n in ("s_scaled", "s_bd", "s_split", "s_zero", "s_sel"))
        pool_passed, dve_passed = sem("pool_passed"), sem("dve_passed")
        x_loaded = sem("x_loaded")
        qkT_mm, v_mm, s_mm, aT_mm, h_mm = (sem(n) for n in ("qkT_mm", "v_mm", "s_mm", "aT_mm", "h_mm"))
        qkT_out, s_masked, s_max, s_neg = (sem(n) for n in ("qkT_out", "s_masked", "s_max", "s_neg"))
        t_exp, t_rcp, t_norm = sem("t_exp"), sem("t_rcp"), sem("t_norm")
        aT_out, v_out, h_out = sem("aT_out"), sem("v_out"), sem("h_out")
        ln1_st, ln1_mv, ln1_ve, ln1_rs, xn_out = (
            sem(n) for n in ("ln1_st", "ln1_mv", "ln1_ve", "ln1_rs", "xn_out"))
        h_kept = sem("h_kept")
        xT_mm, XH_out, XL_out = sem("xT_mm"), sem("XH_out"), sem("XL_out")
        qkv_mm = sem("qkv_mm")
        rot_out = sem("rot_out")
        v1_out, q_out = sem("v1_out"), sem("q_out")
        qT_mm, QH_out, KH_out, QL_out = (sem(n) for n in ("qT_mm", "QH_out", "KH_out", "QL_out"))
        mx_mm, m_out, mT_mm, negm_out = (sem(n) for n in ("mx_mm", "m_out", "mT_mm", "negm_out"))
        st_mm, exp_out = sem("st_mm"), sem("exp_out")
        pv_mm, rden_out, O_out, oT_mm, OT_out = (sem(n) for n in ("pv_mm", "rden_out", "O_out", "oT_mm", "OT_out"))
        y_mm, h2_out = sem("y_mm"), sem("h2_out")
        ln2_st, ln2_mv, ln2_ve, ln2_rs, hn_out = (
            sem(n) for n in ("ln2_st", "ln2_mv", "ln2_ve", "ln2_rs", "hn_out"))
        hT_mm, HH_out, HL_out = sem("hT_mm"), sem("HH_out"), sem("HL_out")
        hid_mm = sem("hid_mm")
        gelu_out = sem("gelu_out")
        ffn_mm, res_out, stored = sem("ffn_mm"), sem("res_out"), sem("stored")

        x_dram = x.rearrange("s (i r) d -> s r i d", i=2)
        block = ctx.enter_context(nc.Block())

        def need(eng, s, value):
            if not isinstance(value, int) or value > 0:
                eng.wait_ge(s, value)

        def wait_apart(eng, passed, *waits):
            for s, v in waits:
                need(eng, s, v)
            eng.sem_inc(passed, 1)

        def run(eng, step):
            step(-1, False, True, False)
            step(0, True, True, False)
            step(1, True, True, True)
            with eng.Fori(2, NP - 1) as p:
                step(p, True, True, True)
            step(NP - 1, True, False, True)
            step(NP, False, False, True)

        @block.sync
        def _(sp):
            for dst, src in ((ident, c_ident), (blk, c_blk), (smask, c_mask), (rope_c, c_rope_c),
                             (rope_s, c_rope_s), (sel_f, c_sel)):
                sp.dma_start(dst[:], src).then_inc(s_const, 16)
            for dst, src in ((wrep[:].rearrange("p j s -> p (j s)"), w_tok), (bias_rows[:], b_tok),
                             (bqk_row[:, 0:P], bq_row)):
                sp.dma_start(dst, src).then_inc(s_w1, 16)

            def step(p, att, tok, ffn):
                if tok:
                    n = p + 1
                    need(sp, h_mm, n)
                    for a in range(2):
                        sp.dma_start(x_sb[:, :, a, :], x_dram[bass.ds(2 * n + a, 1)].rearrange("o r i d -> (o r) i d")
                                     ).then_inc(x_loaded, 16)
                if ffn:
                    n = p - 1
                    sp.wait_ge(res_out, n + 1)
                    sp.dma_start(out[bass.ds(2 * n, 2)].rearrange("a r d -> r a d"), out_sb[:]).then_inc(stored, 16)

            step(-1, False, True, False)
            step(0, True, True, False)
            step(1, True, True, True)
            with sp.Fori(2, NP - 1) as p:
                step(p, True, True, True)
            step(NP - 1, True, False, True)
            step(NP, False, False, True)
            sp.wait_ge(stored, 16 * NP)

        @block.scalar
        def _(act):
            for dst, src in ((w_raw1, w_att1), (w_raw2, w_att2)):
                act.dma_start(dst[:], src).then_inc(s_w2, 16)
            for dst, src in ((win_raw[:, 0:HID], w_in1), (win_raw[:, HID:2 * HID], w_in2), (b_hid[:], b_in),
                             (wo_sb[:], wo.rearrange("(m r) d -> r m d", r=P)),
                             (wout_sb[:], w_out.rearrange("(m r) d -> r m d", r=P))):
                act.dma_start(dst, src).then_inc(s_w3, 16)

            def step(p, att, tok, ffn):
                n = p + 1
                if att:
                    for a in range(2):
                        act.wait_ge(xT_mm, 2 * p + a + 1)
                        need(act, qkv_mm, 6 * (p - 1) + 3 * a + 3)
                        nc.scalar.copy(XH[:, a, :], RING[a][:, 0:DP]).then_inc(XH_out, 1)
                if ffn:
                    act.wait_ge(hT_mm, p)
                    nc.scalar.copy(HH[:].rearrange("p c a t -> p (c a t)"), B6[:]).then_inc(HH_out, 1)
                if ffn:
                    if isinstance(p, int) and p == 1:
                        act.wait_ge(s_w3, 16 * 5)
                    for m in range(NM):
                        act.wait_ge(hid_mm, 3 * (p - 1) + m // 2 + 1)
                        bank = (B7, B6, B7)[m // 2]
                        nc.scalar.activation(G[:, m, :], bank[:, (m % 2) * DP:(m % 2 + 1) * DP], ACT.Gelu,
                                             bias=b_hid[:, m:m + 1]).then_inc(gelu_out, 1)
                if att:
                    for a in range(2):
                        act.wait_ge(qT_mm, 2 * p + a + 1)
                        need(act, st_mm, 6 * (p - 1) + 3 * a + 3)
                        if isinstance(p, int) and p == 0 and a == 0:
                            act.wait_ge(s_zero, 6)
                        for k in range(2):
                            rows = slice(k * HD, (k + 1) * HD)
                            nc.scalar.copy(KH[rows, a, :, k * P:(k + 1) * P], RING[a][rows, 1024:1024 + 2 * DKV].rearrange(
                                "p (g t) -> p g t", g=NKV)).then_inc(KH_out, 1)
                        nc.scalar.copy(QH[:, a, :], RING[a][:, 0:DQ]).then_inc(QH_out, 1)
                if tok:
                    act.wait_ge(v_mm, n + 1)
                    if isinstance(p, int) and p == -1:
                        act.wait_ge(s_w1, 16 * 3)
                    nc.scalar.activation(t_v[:], B6[:, 0:2 * D].rearrange("p (a d) -> p a d", a=2), ACT.Identity,
                                         bias=bias_rows[:, 1:2]).then_inc(v_out, 1)
                    act.wait_ge(s_neg, n + 1)
                    for a in range(2):
                        nc.scalar.activation(t_e[:, a, :], t_s[:, a, :], ACT.Exp, bias=t_neg[:, a:a + 1],
                                             accum_out=t_sum[:, a:a + 1]).then_inc(t_exp, 1)
                if att:
                    for a in range(2):
                        for g in range(NKV):
                            act.wait_ge(st_mm, 6 * p + 3 * a + g + 1)
                            nc.scalar.activation(E[:, a, g, :], RING[a][:, 512 * g:512 * (g + 1)], ACT.Exp,
                                                 scale=SCALE).then_inc(exp_out, 1)
                if tok:
                    act.wait_ge(aT_mm, n + 1)
                    nc.scalar.copy(t_aT[:].rearrange("p a c -> p (a c)"), B7[:, 0:DP]).then_inc(aT_out, 1)
                    act.wait_ge(h_mm, n + 1)
                    need(act, h_kept, n)
                    nc.scalar.activation(h_next[:], B6[:, 0:2 * D].rearrange("p (a d) -> p a d", a=2), ACT.Identity,
                                         bias=bias_sc[:, 0:1]).then_inc(h_out, 1)
                if att:
                    for a in range(2):
                        act.wait_ge(oT_mm, 2 * p + a + 1)
                        nc.scalar.copy(OT[:, a, :], RING[a][:, 0:DQ]).then_inc(OT_out, 1)

            run(act, step)

        @block.gpsimd
        def _(pool):
            nc.gpsimd.memset(half_neg[:], -0.5).then_inc(s_zero, 1)
            nc.gpsimd.memset(v1[:, :, :, HD:HD + 1], 1.0).then_inc(s_zero, 1)
            for zeroed in (KH[:], KL[:]):
                nc.gpsimd.memset(zeroed.bitcast(F32), 0.0).then_inc(s_zero, 1)
            for zeroed in (negmT[:], sel[:]):
                nc.gpsimd.memset(zeroed, 0.0).then_inc(s_zero, 1)


            def normalise(src, mean_var, ve, rs, dst, a):
                nc.gpsimd.tensor_scalar(dst[:, a, 0:D], src[:, a, :], mean_var[:, a, 0:1], rs[:, a:a + 1],
                                        ALU.subtract, ALU.mult)
                return nc.gpsimd.tensor_scalar(dst[:, a, D:DP], src[:, a, P:D], mean_var[:, a, 0:1], rs[:, a:a + 1],
                                               ALU.subtract, ALU.mult)

            def step(p, att, tok, ffn):
                n = p + 1
                if att:
                    wait_apart(pool, pool_passed, (h2_out, 2 * p))
                    nc.gpsimd.tensor_copy(h_cur[:], h_next[:]).then_inc(h_kept, 1)
                    for a in range(2):
                        need(pool, qT_mm, 2 * (p - 1) + a + 1)
                        for b in range(3):
                            pool.wait_ge(rot_out, 6 * p + 3 * a + b + 1)
                            if b < 2:
                                c = slice(b * BANKW, (b + 1) * BANKW)
                                nc.gpsimd.tensor_tensor(q_tok[:, a, c], rot_c[:, a, c], rot_s[:, a, c],
                                                        ALU.add).then_inc(q_out, 1)
                            else:
                                c = slice(DQ, DQ + DKV)
                                kc, ks = (r[:, a, c].rearrange("p (g o d) -> p g o d", g=NKV, o=1)
                                          .broadcast_to([P, NKV, 2, HD]) for r in (rot_c, rot_s))
                                nc.gpsimd.tensor_tensor(k_tok[:, a], kc, ks, ALU.add).then_inc(q_out, 1)
                if tok:
                    wait_apart(pool, pool_passed, (s_max, n + 1))
                    nc.gpsimd.tensor_scalar(t_neg[:], t_max[:], -1.0, None, ALU.mult).then_inc(s_neg, 1)
                    wait_apart(pool, pool_passed, (t_rcp, n + 1))
                    for a in range(2):
                        nc.gpsimd.tensor_scalar(t_a[:, a, :], t_e[:, a, :], t_rs[:, a:a + 1], None,
                                                ALU.mult).then_inc(t_norm, 1)
                    wait_apart(pool, pool_passed, (ln1_mv, 2 * n + 2))
                    nc.gpsimd.tensor_scalar(ve1[:], mv1[:, :, 1], EPS, None, ALU.add).then_inc(ln1_ve, 1)
                    pool.wait_ge(ln1_ve, n + 1)
                    nc.gpsimd.tensor_tensor(rs1[:], ve1[:], half_neg[:], ALU.pow).then_inc(ln1_rs, 1)
                    wait_apart(pool, pool_passed, (ln1_rs, n + 1), (xT_mm, 2 * n))
                    for a in range(2):
                        normalise(h_next, mv1, ve1, rs1, xn, a).then_inc(xn_out, 1)
                if att:
                    need(pool, hT_mm, p)
                    for a in range(2):
                        wait_apart(pool, pool_passed, (ln2_mv, 2 * p + a + 1))
                        nc.gpsimd.tensor_scalar(ve2[:, a:a + 1], mv2[:, a, 1:2], EPS, None, ALU.add).then_inc(ln2_ve, 1)
                        pool.wait_ge(ln2_ve, 2 * p + a + 1)
                        nc.gpsimd.tensor_tensor(rs2[:, a:a + 1], ve2[:, a:a + 1], half_neg[:, 0:1],
                                                ALU.pow).then_inc(ln2_rs, 1)
                        wait_apart(pool, pool_passed, (ln2_rs, 2 * p + a + 1))
                        normalise(h2, mv2, ve2, rs2, hn, a).then_inc(hn_out, 1)

            run(pool, step)

        @block.vector
        def _(dve):
            dve.wait_ge(s_const, 16 * 6)
            dve.wait_ge(s_w1, 16 * 3)
            nc.vector.tensor_scalar(wrep[:, 0, :], wrep[:, 0, :], TOK_SCALE, None, ALU.mult).then_inc(s_scaled, 1)
            nc.vector.tensor_scalar(bias_sc[:], bias_rows[:, 0:1], TOK_SCALE, None, ALU.mult).then_inc(s_scaled, 1)
            nc.vector.tensor_scalar(bqk_row[:, 0:P], bqk_row[:, 0:P], TOK_SCALE, None, ALU.mult).then_inc(s_scaled, 1)
            nc.vector.memset(bqk_row[:, P:DP], 0.0).then_inc(s_scaled, 1)
            dve.wait_ge(s_scaled, 4)
            blk_v = blk[:].rearrange("p (b s) -> p b s", s=T2)
            for j, dst in ((0, bd_qk[:, 0:P // 2]), (1, bd_qk[:, P // 2:P]), (2, bd_v[:])):
                nc.vector.tensor_tensor(dst.rearrange("p (b s) -> p b s", s=T2), blk_v,
                                        wrep[:, j:j + 1, :].broadcast_to([P, 8, T2]), ALU.mult).then_inc(s_bd, 1)
            dve.wait_ge(s_zero, 6)
            nc.vector.tensor_copy(sel[0:NH], sel_f[:]).then_inc(s_sel, 1)
            dve.wait_ge(s_w2, 16 * 2)
            nc.vector.tensor_copy(WH1[:], w_raw1[:]).then_inc(s_split, 1)
            nc.vector.tensor_copy(W2S[:], w_raw2[:]).then_inc(s_split, 1)
            dve.wait_ge(s_split, 2)
            nc.vector.tensor_tensor(WL1[:], w_raw1[:], WH1[:].bitcast(F32), ALU.subtract).then_inc(s_split, 1)
            nc.vector.tensor_tensor(W2S[D2:P, :], w_raw2[D2:P, :], W2S[D2:P, :].bitcast(F32),
                                    ALU.subtract).then_inc(s_split, 1)
            dve.wait_ge(s_w3, 16 * 5)
            nc.vector.tensor_copy(FH1[:], win_raw[:, 0:HID]).then_inc(s_split, 1)
            nc.vector.tensor_copy(F2S[:], win_raw[:, HID:2 * HID]).then_inc(s_split, 1)
            dve.wait_ge(s_split, 6)
            nc.vector.tensor_tensor(FL1[:], win_raw[:, 0:HID], FH1[:].bitcast(F32), ALU.subtract).then_inc(s_split, 1)
            nc.vector.tensor_tensor(F2S[D2:P, :], win_raw[D2:P, HID:2 * HID], F2S[D2:P, :].bitcast(F32),
                                    ALU.subtract).then_inc(s_split, 1)

            def stats(src, st, mv, a, s_st, s_mv, done):
                nc.vector.bn_stats(st[:, a, :], src[:, a, :]).then_inc(s_st, 1)
                wait_apart(dve, dve_passed, (s_st, done))
                nc.vector.bn_aggr(mv[:, a, :], st[:, a, :]).then_inc(s_mv, 1)

            def step(p, att, tok, ffn):
                n = p + 1
                if att:
                    for a in range(2):
                        dve.wait_ge(XH_out, 2 * p + a + 1)
                        nc.vector.tensor_tensor(XL[:, a, :], RING[a][:, 0:DP], XH[:, a, :].bitcast(F32),
                                                ALU.subtract).then_inc(XL_out, 1)
                if ffn:
                    dve.wait_ge(HH_out, p)
                    nc.vector.tensor_tensor(HL[:].rearrange("p c a t -> p (c a t)"), B6[:],
                                            HH[:].rearrange("p c a t -> p (c a t)").bitcast(F32),
                                            ALU.subtract).then_inc(HL_out, 1)
                if att:
                    for a in range(2):
                        need(dve, q_out, 6 * (p - 1) + 3 * a + 3)
                        for b in range(3):
                            heads = 6 if b < 2 else NKV
                            src = RING[a][:, 512 * b:512 * b + heads * HD]
                            c = slice(b * BANKW, b * BANKW + heads * HD)
                            dve.wait_ge(qkv_mm, 6 * p + 3 * a + b + 1)
                            cos = rope_c[:].rearrange("p (o d) -> p o d", o=1).broadcast_to([P, heads, HD])
                            sin = rope_s[:].rearrange("p (o t d) -> p o t d", o=1, t=2).broadcast_to([P, heads, 2, HALF])
                            nc.vector.tensor_tensor(rot_c[:, a, c].rearrange("p (h d) -> p h d", d=HD),
                                                    src.rearrange("p (h d) -> p h d", d=HD), cos, ALU.mult)
                            nc.vector.tensor_tensor(rot_s[:, a, c].rearrange("p (h t d) -> p h t d", t=2, d=HALF),
                                                    src.rearrange("p (h t d) -> p h t d", t=2, d=HALF)[:, :, ::-1, :],
                                                    sin, ALU.mult).then_inc(rot_out, 1)
                        need(dve, pv_mm, 2 * (p - 1) + a + 1)
                        if isinstance(p, int) and p == 0 and a == 0:
                            dve.wait_ge(s_zero, 6)
                        nc.vector.tensor_copy(v1[:, a, :, 0:HD], RING[a][:, 1024 + DKV:1024 + 2 * DKV].rearrange(
                            "p (g d) -> p g d", g=NKV)).then_inc(v1_out, 1)
                    for a in range(2):
                        dve.wait_ge(KH_out, 4 * p + 2 * a + 2)
                        if isinstance(p, int) and p == 0 and a == 0:
                            dve.wait_ge(s_zero, 6)
                        for k in range(2):
                            rows = slice(k * HD, (k + 1) * HD)
                            nc.vector.tensor_tensor(KL[rows, a, :, k * P:(k + 1) * P],
                                                    RING[a][rows, 1024:1024 + 2 * DKV].rearrange("p (g t) -> p g t", g=NKV),
                                                    KH[rows, a, :, k * P:(k + 1) * P].bitcast(F32), ALU.subtract)
                        dve.wait_ge(QH_out, 2 * p + a + 1)
                        nc.vector.tensor_tensor(QL[:, a, :], RING[a][:, 0:DQ], QH[:, a, :].bitcast(F32),
                                                ALU.subtract).then_inc(QL_out, 1)
                if ffn:
                    dve.wait_ge(ffn_mm, 2 * p)
                    need(dve, stored, 16 * (p - 1))
                    nc.vector.tensor_tensor(out_sb[:], B6[:, 0:2 * D].rearrange("p (a d) -> p a d", a=2), h2[:],
                                            ALU.add).then_inc(res_out, 1)
                if tok:
                    dve.wait_ge(qkT_mm, n + 1)
                    if isinstance(p, int) and p == -1:
                        dve.wait_ge(s_bd, 3)
                    nc.vector.tensor_tensor(qkT1[:], B6[:].rearrange("p (a c) -> p a c", a=2),
                                            bqk_row[:].rearrange("p (o c) -> p o c", o=1).broadcast_to([P, 2, DP]), ALU.add)
                    nc.vector.tensor_tensor(qkT2[:], B7[0:D2, :].rearrange("p (a c) -> p a c", a=2),
                                            bqk_row[0:D2, :].rearrange("p (o c) -> p o c", o=1).broadcast_to([D2, 2, DP]),
                                            ALU.add).then_inc(qkT_out, 1)
                if att:
                    for a in range(2):
                        dve.wait_ge(mx_mm, 2 * p + a + 1)
                        nc.vector.reduce_max(m_q[:, a, :], RING[a][:].rearrange("p (h k) -> p h k", k=P),
                                             AX_X).then_inc(m_out, 1)
                    for a in range(2):
                        dve.wait_ge(mT_mm, 2 * p + a + 1)
                        nc.vector.tensor_scalar(negmT[0:NH, a, :], RING[a][0:NH, 0:P], -1.0, None,
                                                ALU.mult).then_inc(negm_out, 1)
                if tok:
                    dve.wait_ge(s_mm, n + 1)
                    nc.vector.tensor_tensor(t_s[:], B7[:, 0:DP].rearrange("p (a c) -> p a c", a=2),
                                            smask[:].rearrange("p (o c) -> p o c", o=1).broadcast_to([P, 2, P]),
                                            ALU.add).then_inc(s_masked, 1)
                    dve.wait_ge(s_masked, n + 1)
                    nc.vector.reduce_max(t_max[:], t_s[:], AX_X).then_inc(s_max, 1)
                    dve.wait_ge(t_exp, 2 * n + 2)
                    nc.vector.reciprocal(t_rs[:], t_sum[:]).then_inc(t_rcp, 1)
                if att:
                    for a in range(2):
                        o_ps = RING[a][:, 0:1024].rearrange("p (b c) -> p b c", b=2)[:, :, 0:6 * (HD + 1)].rearrange(
                            "p b (h e) -> p b h e", e=HD + 1)
                        dve.wait_ge(pv_mm, 2 * p + a + 1)
                        nc.vector.reciprocal(rden[:, a], o_ps[:, :, :, HD]).then_inc(rden_out, 1)
                        dve.wait_ge(rden_out, 2 * p + a + 1)
                        nc.vector.tensor_tensor(O_sb[:, a, :].rearrange("p (b h d) -> p b h d", b=2, h=6),
                                                o_ps[:, :, :, 0:HD],
                                                rden[:, a].rearrange("p b (h o) -> p b h o", o=1).broadcast_to([P, 2, 6, HD]),
                                                ALU.mult).then_inc(O_out, 1)
                if tok:
                    dve.wait_ge(h_out, n + 1)
                    for a in range(2):
                        stats(h_next, st1, mv1, a, ln1_st, ln1_mv, 2 * n + a + 1)
                if att:
                    for a in range(2):
                        dve.wait_ge(y_mm, 2 * p + a + 1)
                        nc.vector.tensor_tensor(h2[:, a, :], RING[a][:, 1024:1024 + D], h_cur[:, a, :],
                                                ALU.add).then_inc(h2_out, 1)
                        dve.wait_ge(h2_out, 2 * p + a + 1)
                        stats(h2, st2, mv2, a, ln2_st, ln2_mv, 2 * p + a + 1)

            run(dve, step)

        @block.tensor
        def _(pe):
            def group(out_ap, terms):
                for i, (lhsT, rhs) in enumerate(terms):
                    last = nc.tensor.matmul(out_ap, lhsT, rhs, start=(i == 0), stop=(i == len(terms) - 1))
                return last

            pe.wait_ge(s_const, 16 * 6)
            pe.wait_ge(s_w3, 16 * 5)
            pe.wait_ge(s_split, 8)
            pe.wait_ge(s_bd, 3)
            pe.wait_ge(s_sel, 1)

            def step(p, att, tok, ffn):
                n = p + 1
                if att:
                    for a in range(2):
                        pe.wait_ge(xn_out, 2 * p + a + 1)
                        need(pe, h2_out, 2 * (p - 1) + a + 1)
                        nc.tensor.transpose(RING[a][:, 0:P], xn[:, a, 0:P], ident[:])
                        nc.tensor.transpose(RING[a][:, P:DP], xn[:, a, P:DP], ident[:]).then_inc(xT_mm, 1)
                if ffn:
                    pe.wait_ge(hn_out, 2 * p)
                    need(pe, h_out, NP if isinstance(p, int) and p >= NP - 1 else p + 1)
                    for c in range(2):
                        for a in range(2):
                            last = nc.tensor.transpose(B6[:, (2 * c + a) * P:(2 * c + a + 1) * P],
                                                       hn[:, a, c * P:(c + 1) * P], ident[:])
                    last.then_inc(hT_mm, 1)
                if att:
                    for a in range(2):
                        pe.wait_ge(XH_out, 2 * p + a + 1)
                        pe.wait_ge(XL_out, 2 * p + a + 1)
                        x1h, x2h, x1l, x2l = XH[:, a, 0:P], XH[:, a, P:DP], XL[:, a, 0:P], XL[:, a, P:DP]
                        for b in range(3):
                            c = slice(b * BANKW, (b + 1) * BANKW)
                            group(RING[a][:, 512 * b:512 * b + BANKW],
                                  ((x1h, WH1[:, c]), (x1h, WL1[:, c]), (x1l, WH1[:, c]),
                                   (x2h, W2S[:, c]), (x2l, W2S[:, c]))).then_inc(qkv_mm, 1)
                if ffn:
                    pe.wait_ge(HH_out, p)
                    pe.wait_ge(HL_out, p)
                    for j, bank in enumerate((B7, B6, B7)):
                        if j == 0:
                            need(pe, aT_out, NP if isinstance(p, int) and p >= NP - 1 else p + 1)
                        if j == 2:
                            pe.wait_ge(gelu_out, 6 * (p - 1) + 2)
                        for m in (2 * j, 2 * j + 1):
                            c = slice(m * P, (m + 1) * P)
                            h1h, h2h = (HH[:, k].rearrange("p a t -> p (a t)") for k in range(2))
                            h1l, h2l = HL[:, 0].rearrange("p a t -> p (a t)"), HL[:, 1].rearrange("p a t -> p (a t)")
                            last = group(bank[:, (m % 2) * DP:(m % 2 + 1) * DP],
                                         ((FH1[:, c], h1h), (FH1[:, c], h1l), (FL1[:, c], h1h),
                                          (F2S[:, c], h2h), (F2S[:, c], h2l)))
                        last.then_inc(hid_mm, 1)
                for a in range(2):
                    if att:
                        pe.wait_ge(q_out, 6 * p + 3 * a + 3)
                        pe.wait_ge(v1_out, 2 * p + a + 1)
                        for t in range(6):
                            nc.tensor.transpose(RING[a][:, t * P:(t + 1) * P], q_tok[:, a, t * P:(t + 1) * P], ident[:])
                        for g in range(NKV):
                            last = nc.tensor.transpose(RING[a][:, 1024 + g * P:1024 + (g + 1) * P],
                                                       k_tok[:, a, g].rearrange("p o d -> p (o d)"), ident[:])
                        last.then_inc(qT_mm, 1)
                    if ffn:
                        pe.wait_ge(gelu_out, 6 * p)
                        group(B6[:, a * D:(a + 1) * D],
                              [(G[:, m, a * P:(a + 1) * P], wout_sb[:, m, :]) for m in range(NM)]).then_inc(ffn_mm, 1)
                if tok:
                    pe.wait_ge(x_loaded, 32 * (n + 1))
                    need(pe, res_out, n - 1)
                    for a in range(2):
                        for i in range(2):
                            dst = B6[:, a * DP:(a + 1) * DP].rearrange("p (k i c) -> p k i c", k=2, i=2)[:, :, i, :]
                            nc.tensor.matmul(dst, x_sb[:, i, a, 0:P], bd_qk[:], start=True, stop=True)
                    for i in range(2):
                        for a in range(2):
                            dst = B7[0:D2, a * DP:(a + 1) * DP].rearrange("p (k i c) -> p k i c", k=2, i=2)[:, :, i, :]
                            last = nc.tensor.matmul(dst, x_sb[:, i, a, P:D],
                                                    bd_qk[:], start=True, stop=True)
                    last.then_inc(qkT_mm, 1)
                if att:
                    for a in range(2):
                        pe.wait_ge(QL_out, 2 * p + a + 1)
                        for t in range(6):
                            last = nc.tensor.matmul(RING[a][:, t * DP:(t + 1) * DP], QH[:, a, t * P:(t + 1) * P],
                                                    KH[:, a, t // 2, :], start=True, stop=True)
                        last.then_inc(mx_mm, 1)
                if tok:
                    pe.wait_ge(qkT_out, n + 1)
                    for i in range(2):
                        last = nc.tensor.matmul(B6[i * D2:(i + 1) * D2, 0:2 * D], bd_v[:],
                                                x_sb[:, i].rearrange("p a d -> p (a d)"), start=True, stop=True)
                    last.then_inc(v_mm, 1)
                    for a in range(2):
                        last = group(B7[:, a * P:(a + 1) * P], (
                            (qkT1[:, a, 0:P], qkT1[:, a, P:DP]), (qkT2[:, a, 0:P], qkT2[:, a, P:DP])))
                    last.then_inc(s_mm, 1)
                if att:
                    for a in range(2):
                        pe.wait_ge(m_out, 2 * p + a + 1)
                        nc.tensor.transpose(RING[a][0:NH, 0:P], m_q[:, a, :], ident[:]).then_inc(mT_mm, 1)
                    for a in range(2):
                        pe.wait_ge(negm_out, 2 * p + a + 1)
                        for g in range(NKV):
                            for odd in range(2):
                                base = 512 * g + odd * DP
                                kh, kl = (k[:, a, g, odd * P:(odd + 1) * P] for k in (KH, KL))
                                qh, ql = (q[:, a, g * DP:(g + 1) * DP] for q in (QH, QL))
                                for i, (lhsT, rhs) in enumerate(((kh, qh), (kl, qh), (kh, ql))):
                                    nc.tensor.matmul(RING[a][:, base:base + DP], lhsT, rhs, start=(i == 0), stop=(i == 2))
                                for t in range(2):
                                    h = REP * g + 2 * t + odd
                                    last = nc.tensor.matmul(RING[a][:, base + t * P:base + (t + 1) * P],
                                                            sel[:, h * P:(h + 1) * P], negmT[:, a, :],
                                                            start=False, stop=True, skip_group_check=True)
                            last.then_inc(st_mm, 1)
                if tok:
                    for a in range(2):
                        pe.wait_ge(t_norm, 2 * n + a + 1)
                        last = nc.tensor.transpose(B7[:, a * P:(a + 1) * P], t_a[:, a, :], ident[:])
                    last.then_inc(aT_mm, 1)
                if att:
                    for a in range(2):
                        for h in range(NH):
                            g, pos = h // REP, (h % 2) * 2 + (h % REP) // 2
                            if h % REP == 0:
                                pe.wait_ge(exp_out, 6 * p + 3 * a + g + 1)
                            col = 512 * (h // 6) + (h % 6) * (HD + 1)
                            last = nc.tensor.matmul(RING[a][:, col:col + HD + 1], E[:, a, g, pos * P:(pos + 1) * P],
                                                    v1[:, a, g, :], start=True, stop=True)
                        last.then_inc(pv_mm, 1)
                if tok:
                    pe.wait_ge(v_out, n + 1)
                    pe.wait_ge(aT_out, n + 1)
                    for i in range(2):
                        nc.tensor.matmul(B6[i * D2:(i + 1) * D2, 0:2 * D], bd_qk[:, 0:P // 2],
                                         x_sb[:, i].rearrange("p a d -> p (a d)"), start=True, stop=False,
                                         skip_group_check=True)
                    for a in range(2):
                        last = nc.tensor.matmul(B6[:, a * D:(a + 1) * D], t_aT[:, a, :], t_v[:, a, :],
                                                start=False, stop=True, skip_group_check=True)
                    last.then_inc(h_mm, 1)
                if att:
                    for a in range(2):
                        pe.wait_ge(O_out, 2 * p + a + 1)
                        for t in range(6):
                            last = nc.tensor.transpose(RING[a][:, t * P:(t + 1) * P], O_sb[:, a, t * P:(t + 1) * P], ident[:])
                        last.then_inc(oT_mm, 1)
                    for a in range(2):
                        pe.wait_ge(OT_out, 2 * p + a + 1)
                        group(RING[a][:, 1024:1024 + D],
                              [(OT[:, a, t * P:(t + 1) * P], wo_sb[:, t, :]) for t in range(6)]).then_inc(y_mm, 1)

            run(pe, step)


def laid_out(x, tok_Wq, tok_bq, tok_Wkv, tok_bkv, Wq, Wk, Wv, Wo, in_weight, in_bias, out_weight):
    w_att = np.concatenate([Wq, Wk, Wv], axis=1)
    w_in = in_weight.T
    return {
        "x": x,
        "w_tok": np.tile(np.concatenate([tok_Wq.T, tok_Wkv.T], axis=1), (P // T, 1)),
        "b_tok": np.tile(np.stack([tok_bq, tok_bkv], axis=1), (P // T2, 1)),
        "bq_row": np.tile(tok_bq[None, :], (P, P // T2)),
        "w_att1": w_att[0:P], "w_att2": np.concatenate([w_att[P:D], w_att[P:D]], axis=0),
        "wo": Wo,
        "w_in1": w_in[0:P], "w_in2": np.concatenate([w_in[P:D], w_in[P:D]], axis=0),
        "b_in": in_bias.reshape(NM, P).T,
        "w_out": out_weight,
    }


_INS = ["x", "L0_tok_Wq", "L0_tok_bq", "L0_tok_Wkv", "L0_tok_bkv", "L0_attn_Wq", "L0_attn_Wk", "L0_attn_Wv",
        "L0_attn_Wo", "L0_ffn_in_weight", "L0_ffn_in_bias", "L0_ffn_out_weight"]


def kernel(**inputs):
    import numpy as _np
    import concourse.bacc as _bacc
    from concourse import mybir as _mybir
    from concourse.bass_utils import run_bass_kernel_spmd as _run

    nc = _bacc.Bacc("TRN2", target_bir_lowering=False, num_devices=1)
    arrays, args = {}, []
    given = laid_out(*(_np.asarray(inputs[name]) for name in _INS))
    for name, a in list(given.items()) + list(const_tables().items()):
        a = _np.ascontiguousarray(a)
        arrays[f"in_{name}_dram"] = a
        args.append(nc.dram_tensor(f"in_{name}_dram", a.shape, _mybir.dt.from_np(a.dtype), kind="ExternalInput").ap())
    out = nc.dram_tensor("out_dram", (64, 128, 192), _mybir.dt.float32, kind="ExternalOutput").ap()
    program(nc, *args, out)
    r = _run(nc, [arrays], core_ids=[0])
    return r.results[0]["out_dram"]
```

```python
from contextlib import ExitStack

import numpy as np

import concourse.bass as bass
from concourse import mybir

ALU = mybir.AluOpType
ACT = mybir.ActivationFunctionType
F32 = mybir.dt.float32
F32R = mybir.dt.float32r
BF16 = mybir.dt.bfloat16
AX_X = mybir.AxisListType.X

P = 128
D = 192
D2 = D - P
DP = 2 * P
T = 16
T2 = T // 2
NH, NKV, HD = 12, 3, 64
REP = NH // NKV
DQ, DKV = NH * HD, NKV * HD
BANKW = 384
HALF = HD // 2
HID = 768
NM = HID // P
SCALE = float(np.float32((HD * 4 / 12) ** -0.5))
TOK_SCALE = float(np.float32(1.0) / np.sqrt(np.float32(D)))
EPS = 1e-5
NEG = -1e30


def const_tables():
    inv = (1.0 / np.power(np.float32(10000.0), np.arange(0, HD, 2, dtype=np.float32) / np.float32(HD))).astype(np.float32)
    fr = np.outer(np.arange(P, dtype=np.float32), inv).astype(np.float32)
    cos, sin = np.cos(fr).astype(np.float32), np.sin(fr).astype(np.float32)
    row = np.arange(P)
    blk = (row[:, None] // T2 == row[None, :] // T2)
    return {
        "ident": np.eye(P, dtype=np.float32),
        "rope_c": np.concatenate([cos, cos], 1),
        "rope_s": np.concatenate([sin, -sin], 1),
        "score_mask": np.where(blk, 0.0, NEG).astype(np.float32),
        "block_ones": (row[:, None] // T == np.arange(P // 2)[None, :] // T2).astype(np.float32),
        "head_sel": np.repeat(np.eye(NH, dtype=np.float32), P, axis=1),
    }


def program(nc, x, w_tok, b_tok, bq_row, w_att1, w_att2, wo, w_in1, w_in2, b_in, w_out,
            c_ident, c_rope_c, c_rope_s, c_mask, c_blk, c_sel, out):
    NSEQ = x.shape[0]
    NP = NSEQ // 2

    with ExitStack() as ctx:
        def sb(name, shape, dt=F32):
            return ctx.enter_context(nc.sbuf_tensor(name, shape, dt))

        def sem(name):
            return ctx.enter_context(nc.semaphore(name))

        RING = [ctx.enter_context(nc.psum_tensor(f"ring{a}", [P, 1536], F32)) for a in range(2)]
        B6 = ctx.enter_context(nc.psum_tensor("bank6", [P, 512], F32))
        B7 = ctx.enter_context(nc.psum_tensor("bank7", [P, 512], F32))

        ident, rope_c, rope_s = sb("ident", [P, P]), sb("rope_c", [P, HD]), sb("rope_s", [P, HD])
        smask, blk = sb("smask", [P, P]), sb("blk", [P, P // 2])
        sel_f, sel = sb("sel_f", [NH, NH * P]), sb("sel", [P, NH * P], BF16)
        half_neg = sb("half_neg", [P, 2])
        wrep = sb("wrep", [P, 3, T2])
        bd_qk, bd_v = sb("bd_qk", [P, P]), sb("bd_v", [P, P // 2])
        bqk_row, bias_rows = sb("bqk_row", [P, DP]), sb("bias_rows", [P, 2])
        bias_sc = sb("bias_sc", [P, 1])
        w_raw1, w_raw2 = sb("w_raw1", [P, 1152]), sb("w_raw2", [P, 1152])
        WH1, WL1, W2S = (sb(n, [P, 1152], F32R) for n in ("WH1", "WL1", "W2S"))
        wo_sb = sb("wo_sb", [P, NM, D])
        win_raw = sb("win_raw", [P, 2 * HID])
        FH1, FL1, F2S = (sb(n, [P, HID], F32R) for n in ("FH1", "FL1", "F2S"))
        b_hid, wout_sb = sb("b_hid", [P, NM]), sb("wout_sb", [P, NM, D])

        x_sb = sb("x_sb", [P, 2, 2, D])
        qkT1, qkT2 = sb("qkT1", [P, 2, DP]), sb("qkT2", [D2, 2, DP])
        t_s, t_e, t_a, t_aT = (sb(n, [P, 2, P]) for n in ("t_s", "t_e", "t_a", "t_aT"))
        t_max, t_neg, t_sum, t_rs = (sb(n, [P, 2]) for n in ("t_max", "t_neg", "t_sum", "t_rs"))
        t_v, h_next, h_cur = (sb(n, [P, 2, D]) for n in ("t_v", "h_next", "h_cur"))
        st1, mv1, ve1, rs1 = sb("st1", [P, 2, 6]), sb("mv1", [P, 2, 2]), sb("ve1", [P, 2]), sb("rs1", [P, 2])
        xn = sb("xn", [P, 2, DP])
        XH, XL = sb("XH", [P, 2, DP], F32R), sb("XL", [P, 2, DP], F32R)
        rot_c, rot_s = sb("rot_c", [P, 2, DQ + DKV]), sb("rot_s", [P, 2, DQ + DKV])
        q_tok, k_tok = sb("q_tok", [P, 2, DQ]), sb("k_tok", [P, 2, NKV, 2, HD])
        QH, QL = sb("QH", [P, 2, DQ], F32R), sb("QL", [P, 2, DQ], F32R)
        KH, KL = sb("KH", [P, 2, NKV, 2 * P], F32R), sb("KL", [P, 2, NKV, 2 * P], F32R)
        m_q, negmT = sb("m_q", [P, 2, NH]), sb("negmT", [P, 2, P], BF16)
        E = sb("E", [P, 2, NKV, 512])
        v1 = sb("v1", [P, 2, NKV, HD + 1])
        rden, O_sb, OT = sb("rden", [P, 2, 2, 6]), sb("O_sb", [P, 2, DQ]), sb("OT", [P, 2, DQ])
        h2 = sb("h2", [P, 2, D])
        st2, mv2, ve2, rs2 = sb("st2", [P, 2, 6]), sb("mv2", [P, 2, 2]), sb("ve2", [P, 2]), sb("rs2", [P, 2])
        hn = sb("hn", [P, 2, DP])
        HH, HL = sb("HH", [P, 2, 2, P], F32R), sb("HL", [P, 2, 2, P], F32R)
        G, out_sb = sb("G", [P, NM, 2 * P]), sb("out_sb", [P, 2, D])

        s_const, s_w1, s_w2, s_w3 = sem("s_const"), sem("s_w1"), sem("s_w2"), sem("s_w3")
        s_scaled, s_bd, s_split, s_zero, s_sel = (
            sem(n) for n in ("s_scaled", "s_bd", "s_split", "s_zero", "s_sel"))
        pool_passed, dve_passed = sem("pool_passed"), sem("dve_passed")
        x_loaded = sem("x_loaded")
        qkT_mm, v_mm, s_mm, aT_mm, h_mm = (sem(n) for n in ("qkT_mm", "v_mm", "s_mm", "aT_mm", "h_mm"))
        qkT_out, s_masked, s_max, s_neg = (sem(n) for n in ("qkT_out", "s_masked", "s_max", "s_neg"))
        t_exp, t_rcp, t_norm = sem("t_exp"), sem("t_rcp"), sem("t_norm")
        aT_out, v_out, h_out = sem("aT_out"), sem("v_out"), sem("h_out")
        ln1_st, ln1_mv, ln1_ve, ln1_rs, xn_out = (
            sem(n) for n in ("ln1_st", "ln1_mv", "ln1_ve", "ln1_rs", "xn_out"))
        h_kept = sem("h_kept")
        xT_mm, XH_out, XL_out = sem("xT_mm"), sem("XH_out"), sem("XL_out")
        qkv_mm = sem("qkv_mm")
        rot_out = sem("rot_out")
        v1_out, q_out = sem("v1_out"), sem("q_out")
        qT_mm, QH_out, KH_out, QL_out = (sem(n) for n in ("qT_mm", "QH_out", "KH_out", "QL_out"))
        mx_mm, m_out, mT_mm, negm_out = (sem(n) for n in ("mx_mm", "m_out", "mT_mm", "negm_out"))
        st_mm, exp_out = sem("st_mm"), sem("exp_out")
        pv_mm, rden_out, O_out, oT_mm, OT_out = (sem(n) for n in ("pv_mm", "rden_out", "O_out", "oT_mm", "OT_out"))
        y_mm, h2_out = sem("y_mm"), sem("h2_out")
        ln2_st, ln2_mv, ln2_ve, ln2_rs, hn_out = (
            sem(n) for n in ("ln2_st", "ln2_mv", "ln2_ve", "ln2_rs", "hn_out"))
        hT_mm, HH_out, HL_out = sem("hT_mm"), sem("HH_out"), sem("HL_out")
        hid_mm = sem("hid_mm")
        gelu_out = sem("gelu_out")
        ffn_mm, res_out, stored = sem("ffn_mm"), sem("res_out"), sem("stored")

        x_dram = x.rearrange("s (i r) d -> s r i d", i=2)
        block = ctx.enter_context(nc.Block())

        def need(eng, s, value):
            if not isinstance(value, int) or value > 0:
                eng.wait_ge(s, value)

        def wait_apart(eng, passed, *waits):
            for s, v in waits:
                need(eng, s, v)
            eng.sem_inc(passed, 1)

        def run(eng, step):
            step(-1, False, True, False)
            step(0, True, True, False)
            step(1, True, True, True)
            with eng.Fori(2, NP - 1) as p:
                step(p, True, True, True)
            step(NP - 1, True, False, True)
            step(NP, False, False, True)

        @block.sync
        def _(sp):
            for dst, src in ((ident, c_ident), (blk, c_blk), (smask, c_mask), (rope_c, c_rope_c),
                             (rope_s, c_rope_s), (sel_f, c_sel)):
                sp.dma_start(dst[:], src).then_inc(s_const, 16)
            for dst, src in ((wrep[:].rearrange("p j s -> p (j s)"), w_tok), (bias_rows[:], b_tok),
                             (bqk_row[:, 0:P], bq_row)):
                sp.dma_start(dst, src).then_inc(s_w1, 16)

            def step(p, att, tok, ffn):
                if tok:
                    n = p + 1
                    need(sp, h_mm, n)
                    for a in range(2):
                        sp.dma_start(x_sb[:, :, a, :], x_dram[bass.ds(2 * n + a, 1)].rearrange("o r i d -> (o r) i d")
                                     ).then_inc(x_loaded, 16)
                if ffn:
                    n = p - 1
                    sp.wait_ge(res_out, n + 1)
                    sp.dma_start(out[bass.ds(2 * n, 2)].rearrange("a r d -> r a d"), out_sb[:]).then_inc(stored, 16)

            step(-1, False, True, False)
            step(0, True, True, False)
            step(1, True, True, True)
            with sp.Fori(2, NP - 1) as p:
                step(p, True, True, True)
            step(NP - 1, True, False, True)
            step(NP, False, False, True)
            sp.wait_ge(stored, 16 * NP)

        @block.scalar
        def _(act):
            for dst, src in ((w_raw1, w_att1), (w_raw2, w_att2)):
                act.dma_start(dst[:], src).then_inc(s_w2, 16)
            for dst, src in ((win_raw[:, 0:HID], w_in1), (win_raw[:, HID:2 * HID], w_in2), (b_hid[:], b_in),
                             (wo_sb[:], wo.rearrange("(m r) d -> r m d", r=P)),
                             (wout_sb[:], w_out.rearrange("(m r) d -> r m d", r=P))):
                act.dma_start(dst, src).then_inc(s_w3, 16)

            def step(p, att, tok, ffn):
                n = p + 1
                if ffn:
                    act.wait_ge(hT_mm, p)
                    nc.scalar.copy(HH[:].rearrange("p c a t -> p (c a t)"), B6[:]).then_inc(HH_out, 1)

                def qk_hi(a):
                    act.wait_ge(qT_mm, 2 * p + a + 1)
                    nc.scalar.copy(QH[:, a, :], RING[a][:, 0:DQ]).then_inc(QH_out, 1)
                    if isinstance(p, int) and p == 0 and a == 0:
                        act.wait_ge(s_zero, 6)
                    for k in range(2):
                        rows = slice(k * HD, (k + 1) * HD)
                        nc.scalar.copy(KH[rows, a, :, k * P:(k + 1) * P], RING[a][rows, 1024:1024 + 2 * DKV].rearrange(
                            "p (g t) -> p g t", g=NKV)).then_inc(KH_out, 1)

                if att and not ffn:
                    qk_hi(0)
                if ffn:
                    if isinstance(p, int) and p == 1:
                        act.wait_ge(s_w3, 16 * 5)
                    for m in range(NM):
                        if att and m == 2:
                            qk_hi(0)
                        act.wait_ge(hid_mm, 3 * (p - 1) + m // 2 + 1)
                        bank = (B7, B6, B7)[m // 2]
                        nc.scalar.activation(G[:, m, :], bank[:, (m % 2) * DP:(m % 2 + 1) * DP], ACT.Gelu,
                                             bias=b_hid[:, m:m + 1]).then_inc(gelu_out, 1)
                if att:
                    qk_hi(1)

                def score_exp(a, g):
                    act.wait_ge(st_mm, 6 * p + 3 * a + g + 1)
                    nc.scalar.activation(E[:, a, g, :], RING[a][:, 512 * g:512 * (g + 1)], ACT.Exp,
                                         scale=SCALE).then_inc(exp_out, 1)

                if att:
                    for g in range(NKV):
                        score_exp(0, g)
                if tok:
                    act.wait_ge(v_mm, n + 1)
                    if isinstance(p, int) and p == -1:
                        act.wait_ge(s_w1, 16 * 3)
                    nc.scalar.activation(t_v[:], B6[:, 0:2 * D].rearrange("p (a d) -> p a d", a=2), ACT.Identity,
                                         bias=bias_rows[:, 1:2]).then_inc(v_out, 1)

                if att:
                    score_exp(1, 0)
                if tok:
                    act.wait_ge(s_neg, n + 1)
                    for a in range(2):
                        nc.scalar.activation(t_e[:, a, :], t_s[:, a, :], ACT.Exp, bias=t_neg[:, a:a + 1],
                                             accum_out=t_sum[:, a:a + 1]).then_inc(t_exp, 1)
                if att:
                    for g in range(1, NKV):
                        score_exp(1, g)
                if tok:
                    act.wait_ge(aT_mm, n + 1)
                    nc.scalar.copy(t_aT[:].rearrange("p a c -> p (a c)"), B7[:, 0:DP]).then_inc(aT_out, 1)
                    act.wait_ge(h_mm, n + 1)
                    need(act, h_kept, n)
                    nc.scalar.activation(h_next[:], B6[:, 0:2 * D].rearrange("p (a d) -> p a d", a=2), ACT.Identity,
                                         bias=bias_sc[:, 0:1]).then_inc(h_out, 1)

                def o_turned(a):
                    act.wait_ge(oT_mm, 2 * p + a + 1)
                    nc.scalar.copy(OT[:, a, :], RING[a][:, 0:DQ]).then_inc(OT_out, 1)

                if att:
                    o_turned(0)
                    o_turned(1)
                if tok:
                    act.wait_ge(xT_mm, n + 1)
                    nc.scalar.copy(XH[:].rearrange("p a c -> p (a c)"), B7[:]).then_inc(XH_out, 1)

            run(act, step)

        @block.gpsimd
        def _(pool):
            nc.gpsimd.memset(half_neg[:], -0.5).then_inc(s_zero, 1)
            nc.gpsimd.memset(v1[:, :, :, HD:HD + 1], 1.0).then_inc(s_zero, 1)
            for zeroed in (KH[:], KL[:]):
                nc.gpsimd.memset(zeroed.bitcast(F32), 0.0).then_inc(s_zero, 1)
            for zeroed in (negmT[:], sel[:]):
                nc.gpsimd.memset(zeroed, 0.0).then_inc(s_zero, 1)


            def step(p, att, tok, ffn):
                n = p + 1

                def rstd2(done, a):
                    wait_apart(pool, pool_passed, (ln2_mv, done))
                    nc.gpsimd.tensor_scalar(ve2[:, a:a + 1], mv2[:, a, 1:2], EPS, None, ALU.add).then_inc(ln2_ve, 1)
                    pool.wait_ge(ln2_ve, done)
                    nc.gpsimd.tensor_tensor(rs2[:, a:a + 1], ve2[:, a:a + 1], half_neg[:, 0:1],
                                            ALU.pow).then_inc(ln2_rs, 1)

                if ffn and not att:
                    rstd2(2 * p, 1)
                if att:
                    for a in range(2):
                        need(pool, qT_mm, 2 * (p - 1) + a + 1)
                        for b in range(3):
                            if ffn and a == 0 and b == 1:
                                rstd2(2 * p, 1)
                            pool.wait_ge(rot_out, 6 * p + 3 * a + b + 1)
                            if b < 2:
                                c = slice(b * BANKW, (b + 1) * BANKW)
                                nc.gpsimd.tensor_tensor(q_tok[:, a, c], rot_c[:, a, c], rot_s[:, a, c],
                                                        ALU.add).then_inc(q_out, 1)
                            else:
                                c = slice(DQ, DQ + DKV)
                                kc, ks = (r[:, a, c].rearrange("p (g o d) -> p g o d", g=NKV, o=1)
                                          .broadcast_to([P, NKV, 2, HD]) for r in (rot_c, rot_s))
                                nc.gpsimd.tensor_tensor(k_tok[:, a], kc, ks, ALU.add).then_inc(q_out, 1)
                    wait_apart(pool, pool_passed, (h2_out, 2 * p))
                    nc.gpsimd.tensor_copy(h_cur[:], h_next[:]).then_inc(h_kept, 1)
                if tok:
                    wait_apart(pool, pool_passed, (s_max, n + 1))
                    nc.gpsimd.tensor_scalar(t_neg[:], t_max[:], -1.0, None, ALU.mult).then_inc(s_neg, 1)
                    wait_apart(pool, pool_passed, (ln1_mv, 2 * n + 2))
                    nc.gpsimd.tensor_scalar(ve1[:], mv1[:, :, 1], EPS, None, ALU.add).then_inc(ln1_ve, 1)
                    pool.wait_ge(ln1_ve, n + 1)
                    nc.gpsimd.tensor_tensor(rs1[:], ve1[:], half_neg[:], ALU.pow).then_inc(ln1_rs, 1)
                if att:
                    rstd2(2 * p + 1, 0)

            run(pool, step)

        @block.vector
        def _(dve):
            dve.wait_ge(s_const, 16 * 6)
            dve.wait_ge(s_w1, 16 * 3)
            nc.vector.tensor_scalar(wrep[:, 0, :], wrep[:, 0, :], TOK_SCALE, None, ALU.mult).then_inc(s_scaled, 1)
            nc.vector.tensor_scalar(bias_sc[:], bias_rows[:, 0:1], TOK_SCALE, None, ALU.mult).then_inc(s_scaled, 1)
            nc.vector.tensor_scalar(bqk_row[:, 0:P], bqk_row[:, 0:P], TOK_SCALE, None, ALU.mult).then_inc(s_scaled, 1)
            nc.vector.memset(bqk_row[:, P:DP], 0.0).then_inc(s_scaled, 1)
            dve.wait_ge(s_scaled, 4)
            blk_v = blk[:].rearrange("p (b s) -> p b s", s=T2)
            for j, dst in ((0, bd_qk[:, 0:P // 2]), (1, bd_qk[:, P // 2:P]), (2, bd_v[:])):
                nc.vector.tensor_tensor(dst.rearrange("p (b s) -> p b s", s=T2), blk_v,
                                        wrep[:, j:j + 1, :].broadcast_to([P, 8, T2]), ALU.mult).then_inc(s_bd, 1)
            dve.wait_ge(s_zero, 6)
            nc.vector.tensor_copy(sel[0:NH], sel_f[:]).then_inc(s_sel, 1)
            dve.wait_ge(s_w2, 16 * 2)
            nc.vector.tensor_copy(WH1[:], w_raw1[:]).then_inc(s_split, 1)
            nc.vector.tensor_copy(W2S[:], w_raw2[:]).then_inc(s_split, 1)
            dve.wait_ge(s_split, 2)
            nc.vector.tensor_tensor(WL1[:], w_raw1[:], WH1[:].bitcast(F32), ALU.subtract).then_inc(s_split, 1)
            nc.vector.tensor_tensor(W2S[D2:P, :], w_raw2[D2:P, :], W2S[D2:P, :].bitcast(F32),
                                    ALU.subtract).then_inc(s_split, 1)
            dve.wait_ge(s_w3, 16 * 5)
            nc.vector.tensor_copy(FH1[:], win_raw[:, 0:HID]).then_inc(s_split, 1)
            nc.vector.tensor_copy(F2S[:], win_raw[:, HID:2 * HID]).then_inc(s_split, 1)
            dve.wait_ge(s_split, 6)
            nc.vector.tensor_tensor(FL1[:], win_raw[:, 0:HID], FH1[:].bitcast(F32), ALU.subtract).then_inc(s_split, 1)
            nc.vector.tensor_tensor(F2S[D2:P, :], win_raw[D2:P, HID:2 * HID], F2S[D2:P, :].bitcast(F32),
                                    ALU.subtract).then_inc(s_split, 1)

            def stats(src, st, mv, a, s_st, s_mv, done):
                nc.vector.bn_stats(st[:, a, :], src[:, a, :]).then_inc(s_st, 1)
                wait_apart(dve, dve_passed, (s_st, done))
                nc.vector.bn_aggr(mv[:, a, :], st[:, a, :]).then_inc(s_mv, 1)

            def normalise(src, mean_var, rs, dst, a):
                nc.vector.tensor_scalar(dst[:, a, 0:D], src[:, a, :], mean_var[:, a, 0:1], rs[:, a:a + 1],
                                        ALU.subtract, ALU.mult)
                return nc.vector.tensor_scalar(dst[:, a, D:DP], src[:, a, P:D], mean_var[:, a, 0:1], rs[:, a:a + 1],
                                               ALU.subtract, ALU.mult)

            def step(p, att, tok, ffn):
                n = p + 1

                def rotate(a, banks):
                    if banks[0] == 0:
                        need(dve, q_out, 6 * (p - 1) + 3 * a + 3)
                    for b in banks:
                        heads = 6 if b < 2 else NKV
                        src = RING[a][:, 512 * b:512 * b + heads * HD]
                        c = slice(b * BANKW, b * BANKW + heads * HD)
                        dve.wait_ge(qkv_mm, 6 * p + 3 * a + b + 1)
                        cos = rope_c[:].rearrange("p (o d) -> p o d", o=1).broadcast_to([P, heads, HD])
                        sin = rope_s[:].rearrange("p (o t d) -> p o t d", o=1, t=2).broadcast_to([P, heads, 2, HALF])
                        nc.vector.tensor_tensor(rot_c[:, a, c].rearrange("p (h d) -> p h d", d=HD),
                                                src.rearrange("p (h d) -> p h d", d=HD), cos, ALU.mult)
                        nc.vector.tensor_tensor(rot_s[:, a, c].rearrange("p (h t d) -> p h t d", t=2, d=HALF),
                                                src.rearrange("p (h t d) -> p h t d", t=2, d=HALF)[:, :, ::-1, :],
                                                sin, ALU.mult).then_inc(rot_out, 1)

                def v_out_of_psum(a):
                    need(dve, pv_mm, 2 * (p - 1) + a + 1)
                    if isinstance(p, int) and p == 0 and a == 0:
                        dve.wait_ge(s_zero, 6)
                    nc.vector.tensor_copy(v1[:, a, :, 0:HD], RING[a][:, 1024 + DKV:1024 + 2 * DKV].rearrange(
                        "p (g d) -> p g d", g=NKV)).then_inc(v1_out, 1)

                def qk_lo(a):
                    dve.wait_ge(QH_out, 2 * p + a + 1)
                    nc.vector.tensor_tensor(QL[:, a, :], RING[a][:, 0:DQ], QH[:, a, :].bitcast(F32), ALU.subtract)
                    dve.wait_ge(KH_out, 4 * p + 2 * a + 2)
                    for k in range(2):
                        rows = slice(k * HD, (k + 1) * HD)
                        last = nc.vector.tensor_tensor(
                            KL[rows, a, :, k * P:(k + 1) * P],
                            RING[a][rows, 1024:1024 + 2 * DKV].rearrange("p (g t) -> p g t", g=NKV),
                            KH[rows, a, :, k * P:(k + 1) * P].bitcast(F32), ALU.subtract)
                    last.then_inc(QL_out, 1)

                def key_max(a):
                    dve.wait_ge(mx_mm, 2 * p + a + 1)
                    nc.vector.reduce_max(m_q[:, a, :], RING[a][:].rearrange("p (h k) -> p h k", k=P),
                                         AX_X).then_inc(m_out, 1)

                def minus_max(a):
                    dve.wait_ge(mT_mm, 2 * p + a + 1)
                    nc.vector.tensor_scalar(negmT[0:NH, a, :], RING[a][0:NH, 0:P], -1.0, None,
                                            ALU.mult).then_inc(negm_out, 1)

                def o_normalised(a):
                    o_ps = RING[a][:, 0:1024].rearrange("p (b c) -> p b c", b=2)[:, :, 0:6 * (HD + 1)].rearrange(
                        "p b (h e) -> p b h e", e=HD + 1)
                    dve.wait_ge(pv_mm, 2 * p + a + 1)
                    nc.vector.reciprocal(rden[:, a], o_ps[:, :, :, HD]).then_inc(rden_out, 1)
                    dve.wait_ge(rden_out, 2 * p + a + 1)
                    nc.vector.tensor_tensor(O_sb[:, a, :].rearrange("p (b h d) -> p b h d", b=2, h=6),
                                            o_ps[:, :, :, 0:HD],
                                            rden[:, a].rearrange("p b (h o) -> p b h o", o=1).broadcast_to([P, 2, 6, HD]),
                                            ALU.mult).then_inc(O_out, 1)

                if att:
                    rotate(0, (0,))
                if ffn:
                    dve.wait_ge(h2_out, 2 * p)
                    stats(h2, st2, mv2, 1, ln2_st, ln2_mv, 2 * p)
                if att:
                    rotate(0, (1,))
                if ffn:
                    dve.wait_ge(ln2_rs, 2 * p)
                    normalise(h2, mv2, rs2, hn, 1).then_inc(hn_out, 1)
                if att:
                    rotate(0, (2,))
                    v_out_of_psum(0)
                    rotate(1, (0,))
                if ffn:
                    dve.wait_ge(HH_out, p)
                    nc.vector.tensor_tensor(HL[:].rearrange("p c a t -> p (c a t)"), B6[:],
                                            HH[:].rearrange("p c a t -> p (c a t)").bitcast(F32),
                                            ALU.subtract).then_inc(HL_out, 1)
                if att:
                    rotate(1, (1, 2))
                    v_out_of_psum(1)
                    qk_lo(0)
                    key_max(0)
                    qk_lo(1)
                    minus_max(0)
                if ffn:
                    dve.wait_ge(ffn_mm, 2 * p)
                    need(dve, stored, 16 * (p - 1))
                    nc.vector.tensor_tensor(out_sb[:], B6[:, 0:2 * D].rearrange("p (a d) -> p a d", a=2), h2[:],
                                            ALU.add).then_inc(res_out, 1)
                if att:
                    key_max(1)
                if tok:
                    dve.wait_ge(qkT_mm, n + 1)
                    if isinstance(p, int) and p == -1:
                        dve.wait_ge(s_bd, 3)
                    nc.vector.tensor_tensor(qkT1[:], B6[:].rearrange("p (a c) -> p a c", a=2),
                                            bqk_row[:].rearrange("p (o c) -> p o c", o=1).broadcast_to([P, 2, DP]), ALU.add)
                    nc.vector.tensor_tensor(qkT2[:], B7[0:D2, :].rearrange("p (a c) -> p a c", a=2),
                                            bqk_row[0:D2, :].rearrange("p (o c) -> p o c", o=1).broadcast_to([D2, 2, DP]),
                                            ALU.add).then_inc(qkT_out, 1)
                if att:
                    minus_max(1)
                if tok:
                    dve.wait_ge(s_mm, n + 1)
                    nc.vector.tensor_tensor(t_s[:], B7[:, 0:DP].rearrange("p (a c) -> p a c", a=2),
                                            smask[:].rearrange("p (o c) -> p o c", o=1).broadcast_to([P, 2, P]),
                                            ALU.add).then_inc(s_masked, 1)
                    dve.wait_ge(s_masked, n + 1)
                    nc.vector.reduce_max(t_max[:], t_s[:], AX_X).then_inc(s_max, 1)
                if tok:
                    dve.wait_ge(t_exp, 2 * n + 2)
                    nc.vector.reciprocal(t_rs[:], t_sum[:]).then_inc(t_rcp, 1)
                    dve.wait_ge(t_rcp, n + 1)
                    for a in range(2):
                        nc.vector.tensor_scalar(t_a[:, a, :], t_e[:, a, :], t_rs[:, a:a + 1], None,
                                                ALU.mult).then_inc(t_norm, 1)
                if att:
                    o_normalised(0)
                    o_normalised(1)
                if tok:
                    dve.wait_ge(h_out, n + 1)
                    for a in range(2):
                        stats(h_next, st1, mv1, a, ln1_st, ln1_mv, 2 * n + a + 1)
                    dve.wait_ge(ln1_rs, n + 1)
                    need(dve, xT_mm, n)
                    for a in range(2):
                        normalise(h_next, mv1, rs1, xn, a).then_inc(xn_out, 1)

                def residual(a):
                    dve.wait_ge(y_mm, 2 * p + a + 1)
                    nc.vector.tensor_tensor(h2[:, a, :], RING[a][:, 1024:1024 + D], h_cur[:, a, :],
                                            ALU.add).then_inc(h2_out, 1)

                if att:
                    dve.wait_ge(h_kept, p + 1)
                    residual(0)
                    dve.wait_ge(h2_out, 2 * p + 1)
                    stats(h2, st2, mv2, 0, ln2_st, ln2_mv, 2 * p + 1)
                if tok:
                    dve.wait_ge(XH_out, n + 1)
                    nc.vector.tensor_tensor(XL[:].rearrange("p a c -> p (a c)"), B7[:],
                                            XH[:].rearrange("p a c -> p (a c)").bitcast(F32),
                                            ALU.subtract).then_inc(XL_out, 1)
                if att:
                    dve.wait_ge(ln2_rs, 2 * p + 1)
                    need(dve, hT_mm, p)
                    normalise(h2, mv2, rs2, hn, 0).then_inc(hn_out, 1)
                    residual(1)

            run(dve, step)

        @block.tensor
        def _(pe):
            def group(out_ap, terms):
                for i, (lhsT, rhs) in enumerate(terms):
                    last = nc.tensor.matmul(out_ap, lhsT, rhs, start=(i == 0), stop=(i == len(terms) - 1))
                return last

            pe.wait_ge(s_const, 16 * 6)
            pe.wait_ge(s_w3, 16 * 5)
            pe.wait_ge(s_split, 8)
            pe.wait_ge(s_bd, 3)
            pe.wait_ge(s_sel, 1)

            def step(p, att, tok, ffn):
                n = p + 1
                toks_done = NP if isinstance(p, int) and p == NP else p + 1

                def qkv(a):
                    need(pe, h2_out, 2 * (p - 1) + a + 1)
                    x1h, x2h, x1l, x2l = XH[:, a, 0:P], XH[:, a, P:DP], XL[:, a, 0:P], XL[:, a, P:DP]
                    for b in range(3):
                        c = slice(b * BANKW, (b + 1) * BANKW)
                        group(RING[a][:, 512 * b:512 * b + BANKW],
                              ((x1h, WH1[:, c]), (x1h, WL1[:, c]), (x1l, WH1[:, c]),
                               (x2h, W2S[:, c]), (x2l, W2S[:, c]))).then_inc(qkv_mm, 1)

                def qk_turned(a):
                    pe.wait_ge(q_out, 6 * p + 3 * a + 3)
                    pe.wait_ge(v1_out, 2 * p + a + 1)
                    for t in range(6):
                        nc.tensor.transpose(RING[a][:, t * P:(t + 1) * P], q_tok[:, a, t * P:(t + 1) * P], ident[:])
                    for g in range(NKV):
                        last = nc.tensor.transpose(RING[a][:, 1024 + g * P:1024 + (g + 1) * P],
                                                   k_tok[:, a, g].rearrange("p o d -> p (o d)"), ident[:])
                    last.then_inc(qT_mm, 1)

                def ffn_second(a):
                    pe.wait_ge(gelu_out, 6 * p)
                    group(B6[:, a * D:(a + 1) * D],
                          [(G[:, m, a * P:(a + 1) * P], wout_sb[:, m, :]) for m in range(NM)]).then_inc(ffn_mm, 1)

                def scores_for_max(a):
                    pe.wait_ge(QL_out, 2 * p + a + 1)
                    for t in range(6):
                        last = nc.tensor.matmul(RING[a][:, t * DP:(t + 1) * DP], QH[:, a, t * P:(t + 1) * P],
                                                KH[:, a, t // 2, :], start=True, stop=True)
                    last.then_inc(mx_mm, 1)

                def max_turned(a):
                    pe.wait_ge(m_out, 2 * p + a + 1)
                    nc.tensor.transpose(RING[a][0:NH, 0:P], m_q[:, a, :], ident[:]).then_inc(mT_mm, 1)

                def scores(a):
                    pe.wait_ge(negm_out, 2 * p + a + 1)
                    for g in range(NKV):
                        for odd in range(2):
                            base = 512 * g + odd * DP
                            kh, kl = (k[:, a, g, odd * P:(odd + 1) * P] for k in (KH, KL))
                            qh, ql = (q[:, a, g * DP:(g + 1) * DP] for q in (QH, QL))
                            for i, (lhsT, rhs) in enumerate(((kh, qh), (kl, qh), (kh, ql))):
                                nc.tensor.matmul(RING[a][:, base:base + DP], lhsT, rhs, start=(i == 0), stop=(i == 2))
                            for t in range(2):
                                h = REP * g + 2 * t + odd
                                last = nc.tensor.matmul(RING[a][:, base + t * P:base + (t + 1) * P],
                                                        sel[:, h * P:(h + 1) * P], negmT[:, a, :],
                                                        start=False, stop=True, skip_group_check=True)
                        last.then_inc(st_mm, 1)

                def probs_v(a):
                    for h in range(NH):
                        g, pos = h // REP, (h % 2) * 2 + (h % REP) // 2
                        if h % REP == 0:
                            pe.wait_ge(exp_out, 6 * p + 3 * a + g + 1)
                        col = 512 * (h // 6) + (h % 6) * (HD + 1)
                        last = nc.tensor.matmul(RING[a][:, col:col + HD + 1], E[:, a, g, pos * P:(pos + 1) * P],
                                                v1[:, a, g, :], start=True, stop=True)
                    last.then_inc(pv_mm, 1)

                def o_turned(a):
                    pe.wait_ge(O_out, 2 * p + a + 1)
                    for t in range(6):
                        last = nc.tensor.transpose(RING[a][:, t * P:(t + 1) * P], O_sb[:, a, t * P:(t + 1) * P], ident[:])
                    last.then_inc(oT_mm, 1)

                def ffn_first():
                    pe.wait_ge(HH_out, p)
                    pe.wait_ge(HL_out, p)
                    for j, bank in enumerate((B7, B6, B7)):
                        if j == 0:
                            pe.wait_ge(XL_out, toks_done)
                        if j == 2:
                            pe.wait_ge(gelu_out, 6 * (p - 1) + 2)
                        for m in (2 * j, 2 * j + 1):
                            c = slice(m * P, (m + 1) * P)
                            h1h, h2h = (HH[:, k].rearrange("p a t -> p (a t)") for k in range(2))
                            h1l, h2l = (HL[:, k].rearrange("p a t -> p (a t)") for k in range(2))
                            last = group(bank[:, (m % 2) * DP:(m % 2 + 1) * DP],
                                         ((FH1[:, c], h1h), (FH1[:, c], h1l), (FL1[:, c], h1h),
                                          (F2S[:, c], h2h), (F2S[:, c], h2l)))
                        last.then_inc(hid_mm, 1)

                def tok_qk():
                    pe.wait_ge(x_loaded, 32 * (n + 1))
                    need(pe, res_out, n - 1)
                    if isinstance(p, int) and p >= 0:
                        need(pe, XL_out, n)
                    for a in range(2):
                        for i in range(2):
                            dst = B6[:, a * DP:(a + 1) * DP].rearrange("p (k i c) -> p k i c", k=2, i=2)[:, :, i, :]
                            nc.tensor.matmul(dst, x_sb[:, i, a, 0:P], bd_qk[:], start=True, stop=True)
                    for i in range(2):
                        for a in range(2):
                            dst = B7[0:D2, a * DP:(a + 1) * DP].rearrange("p (k i c) -> p k i c", k=2, i=2)[:, :, i, :]
                            last = nc.tensor.matmul(dst, x_sb[:, i, a, P:D], bd_qk[:], start=True, stop=True)
                    last.then_inc(qkT_mm, 1)

                def tok_v_scores():
                    pe.wait_ge(qkT_out, n + 1)
                    for i in range(2):
                        last = nc.tensor.matmul(B6[i * D2:(i + 1) * D2, 0:2 * D], bd_v[:],
                                                x_sb[:, i].rearrange("p a d -> p (a d)"), start=True, stop=True)
                    last.then_inc(v_mm, 1)
                    for a in range(2):
                        last = group(B7[:, a * P:(a + 1) * P], (
                            (qkT1[:, a, 0:P], qkT1[:, a, P:DP]), (qkT2[:, a, 0:P], qkT2[:, a, P:DP])))
                    last.then_inc(s_mm, 1)

                def tok_probs_turned():
                    for a in range(2):
                        pe.wait_ge(t_norm, 2 * n + a + 1)
                        last = nc.tensor.transpose(B7[:, a * P:(a + 1) * P], t_a[:, a, :], ident[:])
                    last.then_inc(aT_mm, 1)

                def tok_h():
                    pe.wait_ge(v_out, n + 1)
                    pe.wait_ge(aT_out, n + 1)
                    for i in range(2):
                        nc.tensor.matmul(B6[i * D2:(i + 1) * D2, 0:2 * D], bd_qk[:, 0:P // 2],
                                         x_sb[:, i].rearrange("p a d -> p (a d)"), start=True, stop=False,
                                         skip_group_check=True)
                    for a in range(2):
                        last = nc.tensor.matmul(B6[:, a * D:(a + 1) * D], t_aT[:, a, :], t_v[:, a, :],
                                                start=False, stop=True, skip_group_check=True)
                    last.then_inc(h_mm, 1)

                def x_turned():
                    for a in range(2):
                        pe.wait_ge(xn_out, 2 * n + a + 1)
                        nc.tensor.transpose(B7[:, a * DP:a * DP + P], xn[:, a, 0:P], ident[:])
                        last = nc.tensor.transpose(B7[:, a * DP + P:(a + 1) * DP], xn[:, a, P:DP], ident[:])
                    last.then_inc(xT_mm, 1)

                def hn_turned():
                    pe.wait_ge(hn_out, 2 * p)
                    pe.wait_ge(h_out, toks_done)
                    for c in range(2):
                        for a in range(2):
                            last = nc.tensor.transpose(B6[:, (2 * c + a) * P:(2 * c + a + 1) * P],
                                                       hn[:, a, c * P:(c + 1) * P], ident[:])
                    last.then_inc(hT_mm, 1)

                def output(a):
                    pe.wait_ge(OT_out, 2 * p + a + 1)
                    group(RING[a][:, 1024:1024 + D],
                          [(OT[:, a, t * P:(t + 1) * P], wo_sb[:, t, :]) for t in range(6)]).then_inc(y_mm, 1)

                if att:
                    pe.wait_ge(XH_out, p + 1)
                    pe.wait_ge(XL_out, p + 1)
                    qkv(0)
                    qkv(1)
                if ffn:
                    hn_turned()
                if att:
                    qk_turned(0)
                if ffn:
                    ffn_first()
                if att:
                    qk_turned(1)
                    scores_for_max(0)
                if ffn:
                    ffn_second(0)
                    ffn_second(1)
                if att:
                    max_turned(0)
                    scores_for_max(1)
                if tok:
                    tok_qk()
                if att:
                    scores(0)
                    max_turned(1)
                if tok:
                    tok_v_scores()
                if att:
                    scores(1)
                    probs_v(0)
                if tok:
                    tok_probs_turned()
                if att:
                    probs_v(1)
                if tok:
                    tok_h()
                if att:
                    o_turned(0)
                    o_turned(1)
                    output(0)
                if tok:
                    x_turned()
                if att:
                    output(1)

            run(pe, step)


def laid_out(x, tok_Wq, tok_bq, tok_Wkv, tok_bkv, Wq, Wk, Wv, Wo, in_weight, in_bias, out_weight):
    w_att = np.concatenate([Wq, Wk, Wv], axis=1)
    w_in = in_weight.T
    return {
        "x": x,
        "w_tok": np.tile(np.concatenate([tok_Wq.T, tok_Wkv.T], axis=1), (P // T, 1)),
        "b_tok": np.tile(np.stack([tok_bq, tok_bkv], axis=1), (P // T2, 1)),
        "bq_row": np.tile(tok_bq[None, :], (P, P // T2)),
        "w_att1": w_att[0:P], "w_att2": np.concatenate([w_att[P:D], w_att[P:D]], axis=0),
        "wo": Wo,
        "w_in1": w_in[0:P], "w_in2": np.concatenate([w_in[P:D], w_in[P:D]], axis=0),
        "b_in": in_bias.reshape(NM, P).T,
        "w_out": out_weight,
    }


_INS = ["x", "L0_tok_Wq", "L0_tok_bq", "L0_tok_Wkv", "L0_tok_bkv", "L0_attn_Wq", "L0_attn_Wk", "L0_attn_Wv",
        "L0_attn_Wo", "L0_ffn_in_weight", "L0_ffn_in_bias", "L0_ffn_out_weight"]


def kernel(**inputs):
    import numpy as _np
    import concourse.bacc as _bacc
    from concourse import mybir as _mybir
    from concourse.bass_utils import run_bass_kernel_spmd as _run

    nc = _bacc.Bacc("TRN2", target_bir_lowering=False, num_devices=1)
    arrays, args = {}, []
    given = laid_out(*(_np.asarray(inputs[name]) for name in _INS))
    for name, a in list(given.items()) + list(const_tables().items()):
        a = _np.ascontiguousarray(a)
        arrays[f"in_{name}_dram"] = a
        args.append(nc.dram_tensor(f"in_{name}_dram", a.shape, _mybir.dt.from_np(a.dtype), kind="ExternalInput").ap())
    out = nc.dram_tensor("out_dram", (64, 128, 192), _mybir.dt.float32, kind="ExternalOutput").ap()
    program(nc, *args, out)
    r = _run(nc, [arrays], core_ids=[0])
    return r.results[0]["out_dram"]
```

```python
from contextlib import ExitStack

import numpy as np

import concourse.bass as bass
from concourse import mybir

ALU = mybir.AluOpType
ACT = mybir.ActivationFunctionType
F32 = mybir.dt.float32
F32R = mybir.dt.float32r
BF16 = mybir.dt.bfloat16
AX_X = mybir.AxisListType.X

P = 128
D = 192
D2 = D - P
DP = 2 * P
T = 16
T2 = T // 2
NH, NKV, HD = 12, 3, 64
REP = NH // NKV
DQ, DKV = NH * HD, NKV * HD
BANKW = 384
HALF = HD // 2
HID = 768
NM = HID // P
SCALE = float(np.float32((HD * 4 / 12) ** -0.5))
TOK_SCALE = float(np.float32(1.0) / np.sqrt(np.float32(D)))
EPS = 1e-5
NEG = -1e30


def const_tables():
    inv = (1.0 / np.power(np.float32(10000.0), np.arange(0, HD, 2, dtype=np.float32) / np.float32(HD))).astype(np.float32)
    fr = np.outer(np.arange(P, dtype=np.float32), inv).astype(np.float32)
    cos, sin = np.cos(fr).astype(np.float32), np.sin(fr).astype(np.float32)
    row = np.arange(P)
    token = (row + P // 2) % P
    blk = (token[:, None] // T2 == row[None, :] // T2)
    return {
        "ident": np.eye(P, dtype=np.float32),
        "rope_c": np.concatenate([cos, cos], 1)[token],
        "rope_s": np.concatenate([sin, -sin], 1)[token],
        "score_mask": np.where(blk, 0.0, NEG).astype(np.float32),
        "block_ones": (row[:, None] // T == np.arange(P // 2)[None, :] // T2).astype(np.float32),
        "head_sel": np.repeat(np.eye(NH, dtype=np.float32), P, axis=1),
    }


def program(nc, x, w_tok, b_tok, bq_row, w_att1, w_att2, wo, w_in1, w_in2, b_in, w_out,
            c_ident, c_rope_c, c_rope_s, c_mask, c_blk, c_sel, out):
    NSEQ = x.shape[0]
    NP = NSEQ // 2

    with ExitStack() as ctx:
        def sb(name, shape, dt=F32):
            return ctx.enter_context(nc.sbuf_tensor(name, shape, dt))

        def sem(name):
            return ctx.enter_context(nc.semaphore(name))

        RING = [ctx.enter_context(nc.psum_tensor(f"ring{a}", [P, 1536], F32)) for a in range(2)]
        B6 = ctx.enter_context(nc.psum_tensor("bank6", [P, 512], F32))
        B7 = ctx.enter_context(nc.psum_tensor("bank7", [P, 512], F32))

        ident, rope_c, rope_s = sb("ident", [P, P]), sb("rope_c", [P, HD]), sb("rope_s", [P, HD])
        smask, blk = sb("smask", [P, P]), sb("blk", [P, P // 2])
        sel_f, sel = sb("sel_f", [NH, NH * P]), sb("sel", [P, NH * P], BF16)
        half_neg, warm = sb("half_neg", [P, 2]), sb("warm", [P, 1])
        wrep = sb("wrep", [P, 3, T2])
        bd_qk, bd_vqv = sb("bd_qk", [P, P]), sb("bd_vqv", [P, 3, P // 2])
        bqk_row, bias_rows = sb("bqk_row", [P, DP]), sb("bias_rows", [P, 2])
        bias_sc = sb("bias_sc", [P, 1])
        w_raw1, w_raw2 = sb("w_raw1", [P, 1152]), sb("w_raw2", [P, 1152])
        WH1, WL1, W2S = (sb(n, [P, 1152], F32R) for n in ("WH1", "WL1", "W2S"))
        wo_sb = sb("wo_sb", [P, NM, D])
        win_raw = sb("win_raw", [P, 2 * HID])
        FH1, FL1, F2S = (sb(n, [P, HID], F32R) for n in ("FH1", "FL1", "F2S"))
        b_hid, wout_sb = sb("b_hid", [P, NM]), sb("wout_sb", [P, NM, D])

        x_sb = sb("x_sb", [P, 2, 2, D])
        x2_sb = sb("x2_sb", [P, 2, 2 * D2])
        qkT1, qkT2 = sb("qkT1", [P, 2, DP]), sb("qkT2", [P, DP])
        t_q = sb("t_q", [P, 2, D])
        t_s, t_e, t_a, t_aT = (sb(n, [P, 2, P]) for n in ("t_s", "t_e", "t_a", "t_aT"))
        t_max, t_neg, t_sum, t_rs = (sb(n, [P, 2]) for n in ("t_max", "t_neg", "t_sum", "t_rs"))
        t_v, h_next, h_cur = (sb(n, [P, 2, D]) for n in ("t_v", "h_next", "h_cur"))
        st1, mv1, ve1, rs1 = sb("st1", [P, 2, 6]), sb("mv1", [P, 2, 2]), sb("ve1", [P, 2]), sb("rs1", [P, 2])
        xn = sb("xn", [P, 2, DP])
        XH, XL = sb("XH", [P, 2, DP], F32R), sb("XL", [P, 2, DP], F32R)
        rot_c, rot_s = sb("rot_c", [P, 2, DQ + DKV]), sb("rot_s", [P, 2, DQ + DKV])
        q_tok, k_tok = sb("q_tok", [P, 2, DQ]), sb("k_tok", [P, 2, NKV, 2, HD])
        QH = sb("QH", [P, 2, DQ], F32R)
        QX = sb("QX", [P, 2, 2, DQ], F32R)
        KD = sb("KD", [P, 2, NKV, P], F32R)
        KH, KL = sb("KH", [P, 2, NKV, 2 * P], F32R), sb("KL", [P, 2, NKV, 2 * P], F32R)
        m_q, negmT = sb("m_q", [P, 2, NH]), sb("negmT", [P, 2, P], BF16)
        E = sb("E", [P, 2, NKV, 512])
        v1 = sb("v1", [P, 2, NKV, HD + 1])
        rden, O_sb, OT = sb("rden", [P, 2, 2, 6]), sb("O_sb", [P, 2, DQ]), sb("OT", [P, 2, DQ])
        h2 = sb("h2", [P, 2, D])
        st2, mv2, ve2, rs2 = sb("st2", [P, 2, 6]), sb("mv2", [P, 2, 2]), sb("ve2", [P, 2]), sb("rs2", [P, 2])
        hn = sb("hn", [P, 2, DP])
        HH, HL = sb("HH", [P, 2, 2, P], F32R), sb("HL", [P, 2, 2, P], F32R)
        G, out_sb = sb("G", [P, NM, 2 * P]), sb("out_sb", [P, 2, D])

        s_const, s_w1, s_w2, s_w3 = sem("s_const"), sem("s_w1"), sem("s_w2"), sem("s_w3")
        s_scaled, s_bd, s_hi, s_lo, s_zero, s_sel, s_warm = (
            sem(n) for n in ("s_scaled", "s_bd", "s_hi", "s_lo", "s_zero", "s_sel", "s_warm"))
        pool_passed, dve_passed = sem("pool_passed"), sem("dve_passed")
        x_loaded = sem("x_loaded")
        qkT_mm, s_mm, aT_mm, h_mm = (sem(n) for n in ("qkT_mm", "s_mm", "aT_mm", "h_mm"))
        qkT_out, s_masked, s_max, s_neg = (sem(n) for n in ("qkT_out", "s_masked", "s_max", "s_neg"))
        t_exp, t_rcp, t_norm = sem("t_exp"), sem("t_rcp"), sem("t_norm")
        aT_out, vq_out, h_out = sem("aT_out"), sem("vq_out"), sem("h_out")
        ln1_st, ln1_mv, ln1_ve, ln1_rs, xn_out = (
            sem(n) for n in ("ln1_st", "ln1_mv", "ln1_ve", "ln1_rs", "xn_out"))
        h_kept = sem("h_kept")
        xT_mm, XH_out, XL_out = sem("xT_mm"), sem("XH_out"), sem("XL_out")
        qkv_mm = sem("qkv_mm")
        rot_out = sem("rot_out")
        v1_out, q_out = sem("v1_out"), sem("q_out")
        qT_mm, QH_out, KH_out, QL_out, QX_out = (
            sem(n) for n in ("qT_mm", "QH_out", "KH_out", "QL_out", "QX_out"))
        mx_mm, m_out, mT_mm, negm_out = (sem(n) for n in ("mx_mm", "m_out", "mT_mm", "negm_out"))
        st_mm, exp_out = sem("st_mm"), sem("exp_out")
        pv_mm, rden_out, O_out, oT_mm, OT_out = (sem(n) for n in ("pv_mm", "rden_out", "O_out", "oT_mm", "OT_out"))
        y_mm, h2_out = sem("y_mm"), sem("h2_out")
        ln2_st, ln2_mv, ln2_ve, ln2_rs, hn_out = (
            sem(n) for n in ("ln2_st", "ln2_mv", "ln2_ve", "ln2_rs", "hn_out"))
        hT_mm, HH_out, HL_out = sem("hT_mm"), sem("HH_out"), sem("HL_out")
        hid_mm = sem("hid_mm")
        gelu_out = sem("gelu_out")
        ffn_mm, res_out, stored = sem("ffn_mm"), sem("res_out"), sem("stored")

        x_dram = x.rearrange("s (i r) d -> s r i d", i=2)
        block = ctx.enter_context(nc.Block())

        def need(eng, s, value):
            if not isinstance(value, int) or value > 0:
                eng.wait_ge(s, value)

        def wait_apart(eng, passed, *waits):
            for s, v in waits:
                need(eng, s, v)
            eng.sem_inc(passed, 1)

        def run(eng, step):
            step(-1, False, True, False)
            step(0, True, True, False)
            step(1, True, True, True)
            with eng.Fori(2, NP - 1) as p:
                step(p, True, True, True)
            step(NP - 1, True, False, True)
            step(NP, False, False, True)

        @block.sync
        def _(sp):
            for dst, src in ((wrep[:].rearrange("p j s -> p (j s)"), w_tok), (blk[:], c_blk), (bias_rows[:], b_tok),
                             (bqk_row[:, 0:P], bq_row)):
                sp.dma_start(dst, src).then_inc(s_w1, 16)

            def step(p, att, tok, ffn):
                if tok:
                    n = p + 1
                    need(sp, h_mm, n)
                    for a in range(2):
                        rows = x_dram[bass.ds(2 * n + a, 1)].rearrange("o r i d -> (o r) i d")
                        sp.dma_start(x_sb[:, :, a, :], rows).then_inc(x_loaded, 16)
                        sp.dma_start(x2_sb[:, :, a * D2:(a + 1) * D2], rows[:, :, P:D]).then_inc(x_loaded, 16)
                if ffn:
                    n = p - 1
                    sp.wait_ge(res_out, n + 1)
                    for k in range(2):
                        sp.dma_start(out[bass.ds(2 * n, 2), k * D2:(k + 1) * D2].rearrange("a r d -> r a d"),
                                     out_sb[(1 - k) * D2:(2 - k) * D2]).then_inc(stored, 16)

            step(-1, False, True, False)
            for dst, src in ((smask, c_mask), (ident, c_ident), (rope_c, c_rope_c), (rope_s, c_rope_s), (sel_f, c_sel)):
                sp.dma_start(dst[:], src).then_inc(s_const, 16)
            step(0, True, True, False)
            step(1, True, True, True)
            with sp.Fori(2, NP - 1) as p:
                step(p, True, True, True)
            step(NP - 1, True, False, True)
            step(NP, False, False, True)
            sp.wait_ge(stored, 32 * NP)

        @block.scalar
        def _(act):
            act.wait_ge(x_loaded, 64)
            for dst, src in ((w_raw1, w_att1), (w_raw2, w_att2)):
                act.dma_start(dst[:], src).then_inc(s_w2, 16)
            for dst, src in ((win_raw[:, 0:HID], w_in1), (win_raw[:, HID:2 * HID], w_in2), (b_hid[:], b_in),
                             (wo_sb[:], wo.rearrange("(m r) d -> r m d", r=P)),
                             (wout_sb[:], w_out.rearrange("(m r) d -> r m d", r=P))):
                act.dma_start(dst, src).then_inc(s_w3, 16)
            act.wait_ge(s_w2, 16 * 2)
            nc.scalar.copy(WH1[:], w_raw1[:]).then_inc(s_hi, 1)
            nc.scalar.copy(W2S[:], w_raw2[:]).then_inc(s_hi, 1)

            def step(p, att, tok, ffn):
                n = p + 1
                if ffn:
                    act.wait_ge(hT_mm, p)
                    nc.scalar.copy(HH[:].rearrange("p c a t -> p (c a t)"), B6[:]).then_inc(HH_out, 1)

                def q_hi(a):
                    act.wait_ge(qT_mm, 2 * p + a + 1)
                    nc.scalar.copy(QH[:, a, :], RING[a][:, 0:DQ]).then_inc(QH_out, 1)

                def k_hi(a):
                    if isinstance(p, int) and p == 0 and a == 0:
                        act.wait_ge(s_zero, 6)
                    for k in range(2):
                        rows = slice(k * HD, (k + 1) * HD)
                        nc.scalar.copy(KH[rows, a, :, k * P:(k + 1) * P], RING[a][rows, 1024:1024 + 2 * DKV].rearrange(
                            "p (g t) -> p g t", g=NKV)).then_inc(KH_out, 1)

                if ffn:
                    act.wait_ge(s_warm, p)
                    nc.scalar.activation(warm[:], warm[:], ACT.Gelu).then_inc(s_warm, 1)
                if att:
                    q_hi(0)
                if att and not ffn:
                    k_hi(0)
                if ffn:
                    for m in range(NM):
                        if att and m == 2:
                            k_hi(0)
                        act.wait_ge(hid_mm, 3 * (p - 1) + m // 2 + 1)
                        bank = (B7, B6, B7)[m // 2]
                        nc.scalar.activation(G[:, m, :], bank[:, (m % 2) * DP:(m % 2 + 1) * DP], ACT.Gelu,
                                             bias=b_hid[:, m:m + 1]).then_inc(gelu_out, 1)
                if att:
                    q_hi(1)
                    k_hi(1)
                    for a in range(2):
                        act.wait_ge(KH_out, 4 * p + 2 * a + 2)
                        act.wait_ge(QH_out, 2 * p + a + 1)
                        for k in range(2):
                            own = slice(k * HD, (k + 1) * HD)
                            nc.scalar.copy(QX[own, a, k, :], QH[own, a, :].bitcast(F32)).then_inc(QX_out, 1)
                            nc.scalar.copy(KD[own, a], KH[own, a, :, k * P:(k + 1) * P].bitcast(F32)).then_inc(QX_out, 1)

                def score_exp(a, g):
                    act.wait_ge(st_mm, 6 * p + 3 * a + g + 1)
                    nc.scalar.activation(E[:, a, g, :], RING[a][:, 512 * g:512 * (g + 1)], ACT.Exp,
                                         scale=SCALE).then_inc(exp_out, 1)

                if att:
                    for g in range(NKV):
                        score_exp(0, g)
                if att:
                    score_exp(1, 0)
                if tok:
                    act.wait_ge(s_neg, n + 1)
                    for a in range(2):
                        nc.scalar.activation(t_e[:, a, :], t_s[:, a, :], ACT.Exp, bias=t_neg[:, a:a + 1],
                                             accum_out=t_sum[:, a:a + 1]).then_inc(t_exp, 1)
                    if isinstance(p, int) and p == -1:
                        act.wait_ge(s_scaled, 4)
                    for i, bank in enumerate((B6, B7)):
                        act.wait_ge(s_masked, 2 * n + i + 1)
                        for k, (dst, bias) in enumerate(((t_v, bias_rows[:, 1:2]), (t_q, bias_sc[:]))):
                            r0 = (i ^ k) * (P // 2)
                            rows = slice(r0, r0 + P // 2)
                            nc.scalar.activation(dst[rows], bank[rows, 0:2 * D].rearrange("p (a d) -> p a d", a=2),
                                                 ACT.Identity, bias=bias[rows]).then_inc(vq_out, 1)
                if att:
                    for g in range(1, NKV):
                        score_exp(1, g)
                if tok:
                    act.wait_ge(aT_mm, n + 1)
                    nc.scalar.copy(t_aT[:].rearrange("p a c -> p (a c)"), B7[:, 0:DP]).then_inc(aT_out, 1)

                def o_turned(a):
                    for b, c in enumerate((slice(0, 512), slice(512, DQ))):
                        act.wait_ge(oT_mm, 4 * p + 2 * a + b + 1)
                        nc.scalar.copy(OT[:, a, c], RING[a][:, c]).then_inc(OT_out, 1)

                if att:
                    o_turned(0)
                    o_turned(1)
                if tok:
                    act.wait_ge(xT_mm, n + 1)
                    nc.scalar.copy(XH[:].rearrange("p a c -> p (a c)"), B7[:]).then_inc(XH_out, 1)
                    if isinstance(p, int) and p == -1:
                        act.wait_ge(s_w3, 16 * 5)
                        nc.scalar.copy(FH1[:], win_raw[:, 0:HID]).then_inc(s_hi, 1)
                        nc.scalar.copy(F2S[:], win_raw[:, HID:2 * HID]).then_inc(s_hi, 1)

            run(act, step)

        @block.gpsimd
        def _(pool):
            nc.gpsimd.memset(half_neg[:], -0.5).then_inc(s_zero, 1)
            nc.gpsimd.memset(warm[:], 0.0).then_inc(s_warm, 1)
            nc.gpsimd.memset(v1[:, :, :, HD:HD + 1], 1.0).then_inc(s_zero, 1)
            for zeroed in (KH[:], KL[:]):
                nc.gpsimd.memset(zeroed.bitcast(F32), 0.0).then_inc(s_zero, 1)
            for zeroed in (negmT[:], sel[:]):
                nc.gpsimd.memset(zeroed, 0.0).then_inc(s_zero, 1)


            def step(p, att, tok, ffn):
                n = p + 1

                def rstd2(done, a):
                    wait_apart(pool, pool_passed, (ln2_mv, done))
                    nc.gpsimd.tensor_scalar(ve2[:, a:a + 1], mv2[:, a, 1:2], EPS, None, ALU.add).then_inc(ln2_ve, 1)
                    pool.wait_ge(ln2_ve, done)
                    nc.gpsimd.tensor_tensor(rs2[:, a:a + 1], ve2[:, a:a + 1], half_neg[:, 0:1],
                                            ALU.pow).then_inc(ln2_rs, 1)

                if ffn:
                    rstd2(2 * p, 1)
                if att:
                    for a in range(2):
                        need(pool, qT_mm, 2 * (p - 1) + a + 1)
                        for b in range(3):
                            pool.wait_ge(rot_out, 6 * p + 3 * a + b + 1)
                            if b < 2:
                                c = slice(b * BANKW, (b + 1) * BANKW)
                                nc.gpsimd.tensor_tensor(q_tok[:, a, c], rot_c[:, a, c], rot_s[:, a, c],
                                                        ALU.add).then_inc(q_out, 1)
                            else:
                                c = slice(DQ, DQ + DKV)
                                kc, ks = (r[:, a, c].rearrange("p (g o d) -> p g o d", g=NKV, o=1)
                                          .broadcast_to([P, NKV, 2, HD]) for r in (rot_c, rot_s))
                                nc.gpsimd.tensor_tensor(k_tok[:, a], kc, ks, ALU.add).then_inc(q_out, 1)
                    wait_apart(pool, pool_passed, (h2_out, 2 * p))
                    nc.gpsimd.tensor_copy(h_cur[:], h_next[:]).then_inc(h_kept, 1)
                if tok:
                    wait_apart(pool, pool_passed, (s_max, n + 1))
                    nc.gpsimd.tensor_scalar(t_neg[:], t_max[:], -1.0, None, ALU.mult).then_inc(s_neg, 1)
                    wait_apart(pool, pool_passed, (ln1_mv, 2 * n + 2))
                    nc.gpsimd.tensor_scalar(ve1[:], mv1[:, :, 1], EPS, None, ALU.add).then_inc(ln1_ve, 1)
                    pool.wait_ge(ln1_ve, n + 1)
                    nc.gpsimd.tensor_tensor(rs1[:], ve1[:], half_neg[:], ALU.pow).then_inc(ln1_rs, 1)
                if att:
                    rstd2(2 * p + 1, 0)

            run(pool, step)

        @block.vector
        def _(dve):
            dve.wait_ge(s_w1, 16 * 4)
            nc.vector.tensor_scalar(wrep[:, 0, :], wrep[:, 0, :], TOK_SCALE, None, ALU.mult).then_inc(s_scaled, 1)
            nc.vector.tensor_scalar(bias_sc[:], bias_rows[:, 0:1], TOK_SCALE, None, ALU.mult).then_inc(s_scaled, 1)
            nc.vector.tensor_scalar(bqk_row[:, 0:P], bqk_row[:, 0:P], TOK_SCALE, None, ALU.mult).then_inc(s_scaled, 1)
            nc.vector.memset(bqk_row[:, P:DP], 0.0).then_inc(s_scaled, 1)
            dve.wait_ge(s_scaled, 4)
            blk_v = blk[:].rearrange("p (b s) -> p b s", s=T2)
            for j, dst in ((0, bd_qk[:, 0:P // 2]), (1, bd_qk[:, P // 2:P]),
                           (2, bd_vqv[:, 0]), (0, bd_vqv[:, 1]), (2, bd_vqv[:, 2])):
                nc.vector.tensor_tensor(dst.rearrange("p (b s) -> p b s", s=T2), blk_v,
                                        wrep[:, j:j + 1, :].broadcast_to([P, 8, T2]), ALU.mult).then_inc(s_bd, 1)
            def attention_lo():
                dve.wait_ge(s_hi, 2)
                nc.vector.tensor_tensor(WL1[:], w_raw1[:], WH1[:].bitcast(F32), ALU.subtract).then_inc(s_lo, 1)
                nc.vector.tensor_tensor(W2S[D2:P, :], w_raw2[D2:P, :], W2S[D2:P, :].bitcast(F32),
                                        ALU.subtract).then_inc(s_lo, 1)

            def ffn_lo():
                dve.wait_ge(s_hi, 4)
                nc.vector.tensor_tensor(FL1[:], win_raw[:, 0:HID], FH1[:].bitcast(F32), ALU.subtract).then_inc(s_lo, 1)
                nc.vector.tensor_tensor(F2S[D2:P, :], win_raw[D2:P, HID:2 * HID], F2S[D2:P, :].bitcast(F32),
                                        ALU.subtract).then_inc(s_lo, 1)

            def selectors():
                dve.wait_ge(s_zero, 6)
                nc.vector.tensor_copy(sel[0:NH], sel_f[:]).then_inc(s_sel, 1)

            def stats(src, st, mv, a, s_st, s_mv, done):
                nc.vector.bn_stats(st[:, a, :], src[:, a, :]).then_inc(s_st, 1)
                wait_apart(dve, dve_passed, (s_st, done))
                nc.vector.bn_aggr(mv[:, a, :], st[:, a, :]).then_inc(s_mv, 1)

            def normalise(src, mean_var, rs, dst, a):
                nc.vector.tensor_scalar(dst[:, a, 0:D], src[:, a, :], mean_var[:, a, 0:1], rs[:, a:a + 1],
                                        ALU.subtract, ALU.mult)
                return nc.vector.tensor_scalar(dst[:, a, D:DP], src[:, a, P:D], mean_var[:, a, 0:1], rs[:, a:a + 1],
                                               ALU.subtract, ALU.mult)

            def step(p, att, tok, ffn):
                n = p + 1

                def rotate(a, banks):
                    if banks[0] == 0:
                        need(dve, q_out, 6 * (p - 1) + 3 * a + 3)
                    for b in banks:
                        heads = 6 if b < 2 else NKV
                        src = RING[a][:, 512 * b:512 * b + heads * HD]
                        c = slice(b * BANKW, b * BANKW + heads * HD)
                        dve.wait_ge(qkv_mm, 6 * p + 3 * a + b + 1)
                        cos = rope_c[:].rearrange("p (o d) -> p o d", o=1).broadcast_to([P, heads, HD])
                        sin = rope_s[:].rearrange("p (o t d) -> p o t d", o=1, t=2).broadcast_to([P, heads, 2, HALF])
                        nc.vector.tensor_tensor(rot_c[:, a, c].rearrange("p (h d) -> p h d", d=HD),
                                                src.rearrange("p (h d) -> p h d", d=HD), cos, ALU.mult)
                        nc.vector.tensor_tensor(rot_s[:, a, c].rearrange("p (h t d) -> p h t d", t=2, d=HALF),
                                                src.rearrange("p (h t d) -> p h t d", t=2, d=HALF)[:, :, ::-1, :],
                                                sin, ALU.mult).then_inc(rot_out, 1)

                def v_out_of_psum(a):
                    need(dve, pv_mm, 4 * (p - 1) + 2 * a + 2)
                    if isinstance(p, int) and p == 0 and a == 0:
                        dve.wait_ge(s_zero, 6)
                    nc.vector.tensor_copy(v1[:, a, :, 0:HD], RING[a][:, 1024 + DKV:1024 + 2 * DKV].rearrange(
                        "p (g d) -> p g d", g=NKV)).then_inc(v1_out, 1)

                def qk_lo(a):
                    dve.wait_ge(QH_out, 2 * p + a + 1)
                    for k in range(2):
                        own, other = slice(k * HD, (k + 1) * HD), slice((1 - k) * HD, (2 - k) * HD)
                        nc.vector.tensor_tensor(QX[other, a, k, :], RING[a][own, 0:DQ], QH[own, a, :].bitcast(F32),
                                                ALU.subtract)
                    dve.wait_ge(KH_out, 4 * p + 2 * a + 2)
                    for k in range(2):
                        rows = slice(k * HD, (k + 1) * HD)
                        last = nc.vector.tensor_tensor(
                            KL[rows, a, :, k * P:(k + 1) * P],
                            RING[a][rows, 1024:1024 + 2 * DKV].rearrange("p (g t) -> p g t", g=NKV),
                            KH[rows, a, :, k * P:(k + 1) * P].bitcast(F32), ALU.subtract)
                    last.then_inc(QL_out, 1)

                def key_max(a):
                    dve.wait_ge(mx_mm, 2 * p + a + 1)
                    nc.vector.reduce_max(m_q[:, a, :], RING[a][:].rearrange("p (h k) -> p h k", k=P),
                                         AX_X).then_inc(m_out, 1)

                def minus_max(a):
                    dve.wait_ge(mT_mm, 2 * p + a + 1)
                    nc.vector.tensor_scalar(negmT[0:NH, a, :], RING[a][0:NH, 1024:1024 + P], -1.0, None,
                                            ALU.mult).then_inc(negm_out, 1)

                def o_normalised(a, b):
                    done = 4 * p + 2 * a + b + 1
                    o_ps = RING[a][:, 512 * b:512 * b + 6 * (HD + 1)].rearrange("p (h e) -> p h e", e=HD + 1)
                    dve.wait_ge(pv_mm, done)
                    nc.vector.reciprocal(rden[:, a, b], o_ps[:, :, HD]).then_inc(rden_out, 1)
                    dve.wait_ge(rden_out, done)
                    nc.vector.tensor_tensor(
                        O_sb[:, a, b * BANKW:(b + 1) * BANKW].rearrange("p (h d) -> p h d", h=6), o_ps[:, :, 0:HD],
                        rden[:, a, b].rearrange("p (h o) -> p h o", o=1).broadcast_to([P, 6, HD]),
                        ALU.mult).then_inc(O_out, 1)

                if ffn:
                    dve.wait_ge(h2_out, 2 * p)
                    stats(h2, st2, mv2, 1, ln2_st, ln2_mv, 2 * p)
                if att:
                    rotate(0, (0, 1))
                if ffn:
                    dve.wait_ge(ln2_rs, 2 * p)
                    normalise(h2, mv2, rs2, hn, 1).then_inc(hn_out, 1)
                if att:
                    rotate(0, (2,))
                    v_out_of_psum(0)
                    rotate(1, (0,))
                if ffn:
                    dve.wait_ge(HH_out, p)
                    nc.vector.tensor_tensor(HL[:].rearrange("p c a t -> p (c a t)"), B6[:],
                                            HH[:].rearrange("p c a t -> p (c a t)").bitcast(F32),
                                            ALU.subtract).then_inc(HL_out, 1)
                if att:
                    rotate(1, (1, 2))
                    v_out_of_psum(1)
                    qk_lo(0)
                    qk_lo(1)
                    key_max(0)
                if ffn:
                    dve.wait_ge(ffn_mm, 2 * p)
                    need(dve, stored, 32 * (p - 1))
                    nc.vector.tensor_tensor(out_sb[:], B6[:, 0:2 * D].rearrange("p (a d) -> p a d", a=2), h2[:],
                                            ALU.add).then_inc(res_out, 1)
                if att:
                    minus_max(0)
                if att:
                    key_max(1)
                if tok:
                    dve.wait_ge(qkT_mm, n + 1)
                    if isinstance(p, int) and p == -1:
                        dve.wait_ge(s_bd, 5)
                    nc.vector.tensor_tensor(qkT1[:], B6[:].rearrange("p (a c) -> p a c", a=2),
                                            bqk_row[:].rearrange("p (o c) -> p o c", o=1).broadcast_to([P, 2, DP]), ALU.add)
                    nc.vector.tensor_tensor(qkT2[:], B7[:, 0:DP], bqk_row[:], ALU.add).then_inc(qkT_out, 1)
                if att:
                    minus_max(1)
                if tok:
                    if isinstance(p, int) and p == -1:
                        dve.wait_ge(s_const, 16 * 5)
                    dve.wait_ge(s_mm, n + 1)
                    for a, bank in enumerate((B6, B7)):
                        nc.vector.tensor_tensor(t_s[:, a, :], bank[:, 2 * D:2 * D + P], smask[:],
                                                ALU.add).then_inc(s_masked, 1)
                    dve.wait_ge(s_masked, 2 * n + 2)
                    nc.vector.reduce_max(t_max[:], t_s[:], AX_X).then_inc(s_max, 1)
                if tok:
                    if isinstance(p, int) and p == -1:
                        attention_lo()
                    dve.wait_ge(t_exp, 2 * n + 2)
                    nc.vector.reciprocal(t_rs[:], t_sum[:]).then_inc(t_rcp, 1)
                    dve.wait_ge(t_rcp, n + 1)
                    for a in range(2):
                        nc.vector.tensor_scalar(t_a[:, a, :], t_e[:, a, :], t_rs[:, a:a + 1], None,
                                                ALU.mult).then_inc(t_norm, 1)
                if isinstance(p, int) and p == 0:
                    ffn_lo()
                if att:
                    for a, b in ((0, 0), (0, 1), (1, 0)):
                        o_normalised(a, b)
                if tok:
                    dve.wait_ge(h_mm, n + 1)
                    need(dve, h_kept, n)
                    nc.vector.tensor_tensor(h_next[:], B6[:, 0:2 * D].rearrange("p (a d) -> p a d", a=2), t_q[:],
                                            ALU.add).then_inc(h_out, 1)
                    dve.wait_ge(h_out, n + 1)
                    for a in range(2):
                        nc.vector.bn_stats(st1[:, a, :], h_next[:, a, :]).then_inc(ln1_st, 1)
                if att:
                    o_normalised(1, 1)
                if tok:
                    wait_apart(dve, dve_passed, (ln1_st, 2 * n + 2))
                    for a in range(2):
                        nc.vector.bn_aggr(mv1[:, a, :], st1[:, a, :]).then_inc(ln1_mv, 1)
                    dve.wait_ge(ln1_rs, n + 1)
                    need(dve, xT_mm, n)
                    for a in range(2):
                        normalise(h_next, mv1, rs1, xn, a).then_inc(xn_out, 1)
                    if isinstance(p, int) and p == -1:
                        selectors()

                def residual(a):
                    dve.wait_ge(y_mm, 2 * p + a + 1)
                    nc.vector.tensor_tensor(h2[:, a, :], RING[a][:, 1024:1024 + D], h_cur[:, a, :],
                                            ALU.add).then_inc(h2_out, 1)

                if att:
                    dve.wait_ge(h_kept, p + 1)
                    residual(0)
                    dve.wait_ge(h2_out, 2 * p + 1)
                    stats(h2, st2, mv2, 0, ln2_st, ln2_mv, 2 * p + 1)
                if tok:
                    dve.wait_ge(XH_out, n + 1)
                    nc.vector.tensor_tensor(XL[:].rearrange("p a c -> p (a c)"), B7[:],
                                            XH[:].rearrange("p a c -> p (a c)").bitcast(F32),
                                            ALU.subtract).then_inc(XL_out, 1)
                if att:
                    dve.wait_ge(ln2_rs, 2 * p + 1)
                    need(dve, hT_mm, p)
                    normalise(h2, mv2, rs2, hn, 0).then_inc(hn_out, 1)
                    residual(1)

            run(dve, step)

        @block.tensor
        def _(pe):
            def group(out_ap, terms):
                for i, (lhsT, rhs) in enumerate(terms):
                    last = nc.tensor.matmul(out_ap, lhsT, rhs, start=(i == 0), stop=(i == len(terms) - 1))
                return last

            def step(p, att, tok, ffn):
                n = p + 1
                first = {-1: "tok", 0: "att", 1: "ffn"}.get(p) if isinstance(p, int) else None
                toks_done = NP if isinstance(p, int) and p == NP else p + 1

                def qkv(a, banks=range(3)):
                    need(pe, h2_out, 2 * (p - 1) + a + 1)
                    x1h, x2h, x1l, x2l = XH[:, a, 0:P], XH[:, a, P:DP], XL[:, a, 0:P], XL[:, a, P:DP]
                    for b in banks:
                        c = slice(b * BANKW, (b + 1) * BANKW)
                        group(RING[a][:, 512 * b:512 * b + BANKW],
                              ((x1h, WH1[:, c]), (x1h, WL1[:, c]), (x1l, WH1[:, c]),
                               (x2h, W2S[:, c]), (x2l, W2S[:, c]))).then_inc(qkv_mm, 1)

                def qk_turned(a):
                    pe.wait_ge(q_out, 6 * p + 3 * a + 2)
                    for t in range(6):
                        nc.tensor.transpose(RING[a][:, t * P:(t + 1) * P], q_tok[:, a, t * P:(t + 1) * P], ident[:])
                    pe.wait_ge(q_out, 6 * p + 3 * a + 3)
                    pe.wait_ge(v1_out, 2 * p + a + 1)
                    for g in range(NKV):
                        last = nc.tensor.transpose(RING[a][:, 1024 + g * P:1024 + (g + 1) * P],
                                                   k_tok[:, a, g].rearrange("p o d -> p (o d)"), ident[:])
                    last.then_inc(qT_mm, 1)

                def ffn_second(a):
                    for m in range(NM):
                        if m in (0, 4):
                            pe.wait_ge(gelu_out, 6 * (p - 1) + (4 if m == 0 else 6))
                        last = nc.tensor.matmul(B6[:, a * D:(a + 1) * D], G[:, m, a * P:(a + 1) * P], wout_sb[:, m, :],
                                                start=(m == 0), stop=(m == NM - 1))
                    last.then_inc(ffn_mm, 1)

                def scores_for_max(a):
                    pe.wait_ge(QL_out, 2 * p + a + 1)
                    for t in range(6):
                        last = nc.tensor.matmul(RING[a][:, t * DP:(t + 1) * DP], QH[:, a, t * P:(t + 1) * P],
                                                KH[:, a, t // 2, :], start=True, stop=True)
                    last.then_inc(mx_mm, 1)

                def max_turned(a):
                    pe.wait_ge(m_out, 2 * p + a + 1)
                    nc.tensor.transpose(RING[a][0:NH, 1024:1024 + P], m_q[:, a, :], ident[:]).then_inc(mT_mm, 1)

                def scores(a):
                    pe.wait_ge(QX_out, 8 * p + 4 * a + 4)
                    for g in range(NKV):
                        for odd in range(2):
                            base = 512 * g + odd * DP
                            own = slice(g * DP, (g + 1) * DP)
                            nc.tensor.matmul(RING[a][:, base:base + DP], KD[:, a, g], QX[:, a, odd, own],
                                             start=(odd == 0), stop=False, skip_group_check=True)
                            nc.tensor.matmul(RING[a][:, base:base + DP], KL[:, a, g, odd * P:(odd + 1) * P], QH[:, a, own],
                                             start=False, stop=False, skip_group_check=True)
                        if g == 0:
                            pe.wait_ge(negm_out, 2 * p + a + 1)
                            if first == "att":
                                pe.wait_ge(s_sel, 1)
                        for odd in range(2):
                            base = 512 * g + odd * DP
                            for t in range(2):
                                h = REP * g + 2 * t + odd
                                last = nc.tensor.matmul(RING[a][:, base + t * P:base + (t + 1) * P],
                                                        sel[:, h * P:(h + 1) * P], negmT[:, a, :],
                                                        start=False, stop=True, skip_group_check=True)
                        last.then_inc(st_mm, 1)

                def probs_v(a, heads=range(NH)):
                    for h in heads:
                        g, pos = h // REP, (h % 2) * 2 + (h % REP) // 2
                        if h % REP == 0:
                            pe.wait_ge(exp_out, 6 * p + 3 * a + g + 1)
                        col = 512 * (h // 6) + (h % 6) * (HD + 1)
                        last = nc.tensor.matmul(RING[a][:, col:col + HD + 1], E[:, a, g, pos * P:(pos + 1) * P],
                                                v1[:, a, g, :], start=True, stop=True)
                        if h % 6 == 5:
                            last.then_inc(pv_mm, 1)

                def o_turned(a):
                    for t in range(6):
                        if t % 3 == 0:
                            pe.wait_ge(O_out, 4 * p + 2 * a + t // 3 + 1)
                        last = nc.tensor.transpose(RING[a][:, t * P:(t + 1) * P], O_sb[:, a, t * P:(t + 1) * P], ident[:])
                        if t in (3, 5):
                            last.then_inc(oT_mm, 1)

                def ffn_first():
                    pe.wait_ge(HH_out, p)
                    for j, bank in enumerate((B7, B6, B7)):
                        if j == 0:
                            pe.wait_ge(XL_out, toks_done)
                        if j == 2:
                            pe.wait_ge(gelu_out, 6 * (p - 1) + 2)
                        for m in (2 * j, 2 * j + 1):
                            c = slice(m * P, (m + 1) * P)
                            h1h, h2h = (HH[:, k].rearrange("p a t -> p (a t)") for k in range(2))
                            h1l, h2l = (HL[:, k].rearrange("p a t -> p (a t)") for k in range(2))
                            for i, (w, h) in enumerate(((FH1, h1h), (FL1, h1h), (F2S, h2h), (FH1, h1l), (F2S, h2l))):
                                if m == 0 and i == 3:
                                    pe.wait_ge(HL_out, p)
                                last = nc.tensor.matmul(bank[:, (m % 2) * DP:(m % 2 + 1) * DP], w[:, c], h,
                                                        start=(i == 0), stop=(i == 4))
                        last.then_inc(hid_mm, 1)

                qk_columns = (slice(1, 3), slice(0, 4, 3))

                def tok_qk_rest():
                    pe.wait_ge(x_loaded, 64 * (n + 1))
                    if isinstance(p, int) and p >= 0:
                        need(pe, XL_out, n)
                    for i in range(2):
                        dst = B7[:, 0:DP].rearrange("p (b c) -> p b c", b=4)[:, qk_columns[i]]
                        nc.tensor.matmul(dst, x2_sb[:, i], bd_qk[:], start=True, stop=True)

                def tok_qk():
                    need(pe, res_out, n - 1)
                    for i in range(2):
                        for a in range(2):
                            dst = B6[:, a * DP:(a + 1) * DP].rearrange("p (b c) -> p b c", b=4)[:, qk_columns[i]]
                            last = nc.tensor.matmul(dst, x_sb[:, i, a, 0:P], bd_qk[:], start=True, stop=True)
                    last.then_inc(qkT_mm, 1)

                def tok_v_scores():
                    pe.wait_ge(qkT_out, n + 1)
                    for i, bank in enumerate((B6, B7)):
                        nc.tensor.matmul(bank[:, 0:2 * D], bd_vqv[:, i:i + 2].rearrange("p b c -> p (b c)"),
                                         x_sb[:, i].rearrange("p a d -> p (a d)"), start=True, stop=True)
                    for a, bank in enumerate((B6, B7)):
                        own = slice(a * D2, (a + 1) * D2)
                        last = group(bank[:, 2 * D:2 * D + P], (
                            (qkT1[:, a, 0:P], qkT1[:, a, P:DP]), (qkT2[own, 0:P], qkT2[own, P:DP])))
                    last.then_inc(s_mm, 1)

                def tok_probs_turned():
                    pe.wait_ge(vq_out, 4 * n + 4)
                    if first == "tok":
                        pe.wait_ge(s_const, 16 * 5)
                    for a in range(2):
                        pe.wait_ge(t_norm, 2 * n + a + 1)
                        last = nc.tensor.transpose(B7[:, a * P:(a + 1) * P], t_a[:, a, :], ident[:])
                    last.then_inc(aT_mm, 1)

                def tok_h():
                    pe.wait_ge(aT_out, n + 1)
                    for a in range(2):
                        last = nc.tensor.matmul(B6[:, a * D:(a + 1) * D], t_aT[:, a, :], t_v[:, a, :],
                                                start=True, stop=True)
                    last.then_inc(h_mm, 1)

                def x_turned():
                    for a in range(2):
                        pe.wait_ge(xn_out, 2 * n + a + 1)
                        nc.tensor.transpose(B7[:, a * DP:a * DP + P], xn[:, a, 0:P], ident[:])
                        last = nc.tensor.transpose(B7[:, a * DP + P:(a + 1) * DP], xn[:, a, P:DP], ident[:])
                    last.then_inc(xT_mm, 1)

                def hn_turned():
                    pe.wait_ge(hn_out, 2 * p)
                    pe.wait_ge(h_out, toks_done)
                    for c in range(2):
                        for a in range(2):
                            last = nc.tensor.transpose(B6[:, (2 * c + a) * P:(2 * c + a + 1) * P],
                                                       hn[:, a, c * P:(c + 1) * P], ident[:])
                    last.then_inc(hT_mm, 1)

                def output(a):
                    if first == "att":
                        pe.wait_ge(s_w3, 16 * 5)
                    for t in range(6):
                        if t % 4 == 0:
                            pe.wait_ge(OT_out, 4 * p + 2 * a + t // 4 + 1)
                        last = nc.tensor.matmul(RING[a][:, 1024:1024 + D], OT[:, a, t * P:(t + 1) * P], wo_sb[:, t, :],
                                                start=(t == 0), stop=(t == 5))
                    last.then_inc(y_mm, 1)

                if first == "tok":
                    pe.wait_ge(s_bd, 5)
                if first == "att":
                    pe.wait_ge(s_lo, 2)
                if first == "ffn":
                    pe.wait_ge(s_lo, 4)
                if att:
                    pe.wait_ge(XH_out, p + 1)
                    pe.wait_ge(XL_out, p + 1)
                    qkv(0)
                    qkv(1, (0, 1))
                if ffn:
                    hn_turned()
                if att:
                    qkv(1, (2,))
                if att:
                    qk_turned(0)
                if ffn:
                    ffn_first()
                if att:
                    qk_turned(1)
                if ffn:
                    ffn_second(0)
                if att:
                    scores_for_max(0)
                if ffn:
                    ffn_second(1)
                if att:
                    scores_for_max(1)
                if tok:
                    tok_qk_rest()
                if att:
                    max_turned(0)
                if tok:
                    tok_qk()
                if att:
                    scores(0)
                    max_turned(1)
                if tok:
                    tok_v_scores()
                if att:
                    scores(1)
                    probs_v(0)
                if tok:
                    tok_probs_turned()
                if att:
                    probs_v(1, range(0, 6))
                if tok:
                    tok_h()
                if att:
                    probs_v(1, range(6, NH))
                    o_turned(0)
                    o_turned(1)
                    output(0)
                if tok:
                    x_turned()
                if att:
                    output(1)

            run(pe, step)


def laid_out(x, tok_Wq, tok_bq, tok_Wkv, tok_bkv, Wq, Wk, Wv, Wo, in_weight, in_bias, out_weight):
    w_att = np.concatenate([Wq, Wk, Wv], axis=1)
    w_in = in_weight.T
    return {
        "x": x,
        "w_tok": np.tile(np.concatenate([tok_Wq.T, tok_Wkv.T], axis=1), (P // T, 1)),
        "b_tok": np.tile(np.stack([tok_bq, tok_bkv], axis=1), (P // T2, 1)),
        "bq_row": np.tile(tok_bq[None, :], (P, P // T2)),
        "w_att1": w_att[0:P], "w_att2": np.concatenate([w_att[P:D], w_att[P:D]], axis=0),
        "wo": Wo,
        "w_in1": w_in[0:P], "w_in2": np.concatenate([w_in[P:D], w_in[P:D]], axis=0),
        "b_in": in_bias.reshape(NM, P).T,
        "w_out": out_weight,
    }


_INS = ["x", "L0_tok_Wq", "L0_tok_bq", "L0_tok_Wkv", "L0_tok_bkv", "L0_attn_Wq", "L0_attn_Wk", "L0_attn_Wv",
        "L0_attn_Wo", "L0_ffn_in_weight", "L0_ffn_in_bias", "L0_ffn_out_weight"]


def kernel(**inputs):
    import numpy as _np
    import concourse.bacc as _bacc
    from concourse import mybir as _mybir
    from concourse.bass_utils import run_bass_kernel_spmd as _run

    nc = _bacc.Bacc("TRN2", target_bir_lowering=False, num_devices=1)
    arrays, args = {}, []
    given = laid_out(*(_np.asarray(inputs[name]) for name in _INS))
    for name, a in list(given.items()) + list(const_tables().items()):
        a = _np.ascontiguousarray(a)
        arrays[f"in_{name}_dram"] = a
        args.append(nc.dram_tensor(f"in_{name}_dram", a.shape, _mybir.dt.from_np(a.dtype), kind="ExternalInput").ap())
    out = nc.dram_tensor("out_dram", (64, 128, 192), _mybir.dt.float32, kind="ExternalOutput").ap()
    program(nc, *args, out)
    r = _run(nc, [arrays], core_ids=[0])
    return r.results[0]["out_dram"]
```
